# Optimizing a Trainium2 kernel written in Bass

```python
import numpy as np
import jax
import jax.numpy as jnp

def _softmax(x, axis=-1):
    return jax.nn.softmax(x, axis=axis)

def _gelu(x):
    return jax.nn.gelu(x, approximate=True)

def _silu(x):
    return jax.nn.silu(x)

def _sigmoid(x):
    return jax.nn.sigmoid(x)

def _layernorm(x, axis=-1, eps=1e-05):
    m = jnp.mean(x, axis=axis, keepdims=True)
    v = jnp.var(x, axis=axis, keepdims=True)
    return (x - m) / jnp.sqrt(v + eps)

def _scatter_add(tgt, idx, src, axis=0):
    return tgt.at[idx].add(src)

def _segment_sum(src, seg, n):
    return jax.ops.segment_sum(src, seg, n)
kernel_name = 'mk_gnn_resnorm_d1_gnn_r16_bf87d7'

def setup_inputs(seed: int=0):
    np.random.seed(seed)
    _w = jnp.asarray

    def _rec_inputs():
        import jax
        import jax.numpy as jnp
        _gk = jax.random.key(seed)
        x = 0.0002542 + 0.9999 * jax.random.normal(jax.random.fold_in(_gk, 1), (6250, 128), jnp.float32)
        src = jax.random.randint(jax.random.fold_in(_gk, 2), (100000,), 0, 6250, jnp.int32)
        dst = jnp.minimum((6250 * jax.random.uniform(jax.random.fold_in(_gk, 3), (100000,)) ** 2.0).astype(jnp.int32), 99999)
        _o = jnp.argsort(dst, stable=True)
        src = src[_o]
        dst = dst[_o]
        edge_type_4 = jax.random.randint(jax.random.fold_in(_gk, 12), (100000,), 0, 4, jnp.int32)
        return (x, src, dst, edge_type_4)
    x, src, dst, edge_type_4 = _rec_inputs()

    def _L0_gnn_setup():
        import jax, jax.numpy as jnp
        import numpy as np
        N_NODES = 6250
        N_EDGES = 40000
        D = 128
        N_REL = 4
        N_LAYERS = 3

        def _rgcn_conv(x, edge_index, edge_type, W, root, bias):
            src, dst = (edge_index[0], edge_index[1])
            x_src = x[src]
            out = x @ root + bias
            for r in range(N_REL):
                mask = (edge_type == r).astype(x.dtype)
                s = jax.ops.segment_sum(x_src * mask[:, None], dst, num_segments=N_NODES)
                c = jax.ops.segment_sum(mask, dst, num_segments=N_NODES)
                mean = s / jnp.maximum(c, 1.0)[:, None]
                out = out + mean @ W[r]
            return out
        key = jax.random.key(seed)
        k = jax.random.split(key, 6)
        edge_index = jax.random.randint(k[0], (2, N_EDGES), 0, N_NODES, dtype=jnp.int32)
        edge_type = jax.random.randint(k[1], (N_EDGES,), 0, N_REL, dtype=jnp.int32)
        x_init = jax.random.normal(k[2], (N_NODES, D), dtype=jnp.float32)
        scale = 1.0 / np.sqrt(D)
        weights = jax.random.normal(k[3], (N_LAYERS, N_REL, D, D), dtype=jnp.float32) * scale
        roots = jax.random.normal(k[4], (N_LAYERS, D, D), dtype=jnp.float32) * scale
        biases = jax.random.normal(k[5], (N_LAYERS, D), dtype=jnp.float32) * 0.01
        return {'edge_index': edge_index, 'edge_type': edge_type, 'x_init': x_init, 'weights': weights, 'roots': roots, 'biases': biases}
    _L0_gnn_all = _L0_gnn_setup()
    _L0_gnn_in = {k: v for k, v in _L0_gnn_all.items() if k in ('weights', 'roots', 'biases')}
    del _L0_gnn_all
    return {'x': x, 'src': src, 'dst': dst, 'edge_type_4': edge_type_4, 'L0_gnn_weights': _L0_gnn_in['weights'], 'L0_gnn_roots': _L0_gnn_in['roots'], 'L0_gnn_biases': _L0_gnn_in['biases']}

def reference(x, src, dst, edge_type_4, L0_gnn_weights, L0_gnn_roots, L0_gnn_biases):
    import jax
    import jax.numpy as jnp

    def _L0_gnn_ref(edge_index, edge_type, x_init, weights, roots, biases):
        import jax, jax.numpy as jnp
        import numpy as np
        N_NODES = 6250
        N_EDGES = 40000
        D = 128
        N_REL = 4
        N_LAYERS = 3

        def _rgcn_conv(x, edge_index, edge_type, W, root, bias):
            src, dst = (edge_index[0], edge_index[1])
            x_src = x[src]
            out = x @ root + bias
            for r in range(N_REL):
                mask = (edge_type == r).astype(x.dtype)
                s = jax.ops.segment_sum(x_src * mask[:, None], dst, num_segments=N_NODES)
                c = jax.ops.segment_sum(mask, dst, num_segments=N_NODES)
                mean = s / jnp.maximum(c, 1.0)[:, None]
                out = out + mean @ W[r]
            return out
        x = x_init
        for l in range(N_LAYERS - 1):
            x = _rgcn_conv(x, edge_index, edge_type, weights[l], roots[l], biases[l])
            x = jax.nn.relu(x)
        x = _rgcn_conv(x, edge_index, edge_type, weights[-1], roots[-1], biases[-1])
        return x
    edge_index = jnp.stack([src, dst])
    x = _layernorm(x + _L0_gnn_ref(edge_index, edge_type_4, x, L0_gnn_weights, L0_gnn_roots, L0_gnn_biases), axis=-1)
    return x

_drawn_inputs = setup_inputs


def setup_inputs(seed=0):
    import zlib

    import numpy as np

    out = dict(_drawn_inputs(seed))
    spreads = {}
    factors = {'L0_gnn_biases': 7.639}
    for name, (base, spread) in spreads.items():
        noise = np.random.default_rng([zlib.crc32(name.encode()), seed]).standard_normal(out[name].shape)
        drawn = base * np.exp(spread * noise) if base else spread * noise
        out[name] = jnp.asarray(drawn.astype(out[name].dtype))
    for name, factor in factors.items():
        out[name] = (out[name] * factor).astype(out[name].dtype)
    return out
```

```python
import numpy as np
import concourse.bass as bass
import concourse.mybir as mybir
from contextlib import ExitStack

F32 = mybir.dt.float32
I32 = mybir.dt.int32
ALU = mybir.AluOpType
ACT = mybir.ActivationFunctionType
AX = mybir.AxisListType

P = 128
D = 128
NR = 4
NL = 3
RW = 1024
FAR = 1000000
EPS = 1e-5


def sizes(N, E):
    NP = -(-E // RW)
    NG = -(-E // 512)
    NT = -(-E // P)
    NB = -(-N // P)
    need = [max(0, int((N * (g / NG) ** 2 - 96) // P)) for g in range(2 * NP)]
    return NP, NG, NT, NB, need


def constants(N, E):
    NP, NG, NT, NB, need = sizes(N, E)
    e = np.arange(P, dtype=np.float32)
    valid = (np.arange(NP * RW).reshape(NP, RW) < E).astype(np.float32)
    return {
        "c_ident": np.eye(P, dtype=np.float32),
        "c_iota": np.tile(e, (P, 1)),
        "c_lower": (e[None, :] < e[:, None]).astype(np.float32),
        "c_col": np.stack([N + e, NR * N + e], 1).astype(np.float32),
        "c_valid": valid,
        "c_need": (P * np.array(need, np.float32)).reshape(NP, 2),
    }


def rgcn_kernel(nc, x, src, dst, typ, weights, roots, biases, c_ident, c_iota, c_lower, c_col, c_valid, c_need, out):
    N, E = x.shape[0], src.shape[0]
    NP, NG, NT, NB, need = sizes(N, E)
    NT4 = NP * 8
    NW = NB * P + P
    NK = NR * N
    R = 14
    NS = 3
    YS = 4
    FULL = E // RW
    REST = E - FULL * RW
    bw = [min(P, N - k * P) for k in range(NB)]

    after, done = [], 0
    for g in range(NG - 1):
        k = min(need[g + 1], NB)
        after.append(list(range(done, k)))
        done = max(done, k)
    after.append(list(range(done, NB)))
    group_of = {k: g for g in range(NG) for k in after[g]}
    tiles = [[t for t in range(4 * g, 4 * g + 4) if t < NT] for g in range(NG)]
    rows_of = [min(P, E - t * P) for t in range(NT)]

    ctx = ExitStack()
    with ctx:
        sb = lambda name, shape, dt=F32: ctx.enter_context(nc.sbuf_tensor(name, shape, dt))
        ps = lambda name, shape: ctx.enter_context(nc.psum_tensor(name, shape, F32))
        sem = lambda name: ctx.enter_context(nc.semaphore(name))
        ctx.enter_context(nc.allow_non_contiguous_dma("the biases, one element a partition"))

        Y = [nc.dram_tensor(f"ytab{i}", [NK, D], F32).ap() for i in range(2)]
        acc_dram = nc.dram_tensor("acc_dram", [(NB + 1) * P, D], F32).ap()
        NC = -(-(NK + P) // P)
        cnt_dram = nc.dram_tensor("cnt_dram", [NC * P, 1], F32).ap()

        ident, iota, lower = sb("ident", [P, P]), sb("iota", [P, P]), sb("lower", [P, P])
        dumpc = sb("dumpc", [P, 2])
        need_t = sb("need_t", [NP, 2])
        valid = sb("valid", [NP, RW])
        a_dst, a_prev, a_next = sb("a_dst", [NP, RW], I32), sb("a_prev", [NP, RW], I32), sb("a_next", [NP, RW], I32)
        a_src, a_typ = sb("a_src", [NP, RW], I32), sb("a_typ", [NP, RW], I32)
        a_idx, a_rel, a_w = sb("a_idx", [NP, RW]), sb("a_rel", [NP, RW]), sb("a_w", [NP, RW])
        same_p, same_n = sb("same_p", [NP, RW]), sb("same_n", [NP, RW])
        mask, fwd, bwd = sb("mask", [NP, RW]), sb("fwd", [NP, RW]), sb("bwd", [NP, RW])
        ends = sb("ends", [NP, 2, 2, NR])
        rowt = sb("rowt", [NR, 2, 2, NP + 2])
        carry = sb("carry", [NR, 2, NP + 2])
        cin = sb("cin", [NP, 2, NR])
        chk = sb("chk", [NP, 8])
        ones = sb("ones", [P, 1])
        flag_i = sb("flag_i", [1, 1], I32)
        brow = sb("brow", [1, 2, NP], I32)
        idxc = sb("idxc", [P, NT4], I32)
        relc, wc = sb("relc", [P, NT4]), sb("wc", [P, NT4])
        B = [sb("node0", [P, NW]), sb("node1", [P, NW])]
        xn = sb("xn", [P, NB, D])
        wt = sb("wt", [P, NL, NR, D])
        rt = sb("rt", [P, NL, D])
        bt = sb("bt", [P, NL])
        ring = sb("ring", [P, R * 512])
        S = sb("S", [P, NS, 4, P])
        yst = sb("yst", [P, YS, NR * D])
        zt = sb("zt", [P, 2, 4, D])
        st = sb("st", [P, 4, 6])
        mv = sb("mv", [P, 4, 2])
        sd = sb("sd", [P, 4])
        rs = sb("rs", [P, 4])
        epst = sb("epst", [P, 1])

        psG = [ps("psG0", [P, 512]), ps("psG1", [P, 512])]
        psY = [ps("psY0", [P, 512]), ps("psY1", [P, 512])]
        psR = [ps("psR0", [P, 512]), ps("psR1", [P, 512])]
        psT = [ps("psT0", [P, 512]), ps("psT1", [P, 512])]

        names = ("s_e0 s_e1 s_c s_x s_w s_fill s_v s_xt s_ym s_rm s_yev s_rev s_st s_tp s_fl s_carry s_tev "
                 "s_S s_pe s_acc s_relu s_fin s_va s_sq s_no tSP tPE tACT tDVE tPOOL gd gp s_br s_v2").split()
        q = {n: sem(n) for n in names}
        s_ring = [sem(f"s_ring{i}") for i in range(R)]
        s_yd = [sem(f"s_yd{i}") for i in range(YS)]
        s_od = [sem(f"s_od{i}") for i in range(2)]
        block = ctx.enter_context(nc.Block())

        base_ap = brow[:].rearrange("a h p -> a (h p)")
        base_col = lambda g: (g % 2) * NP + g // 2
        dview = dst.rearrange("(a e) -> a e", a=1)

        def node_src(li):
            return B[li % 2], B[(li + 1) % 2]

        def sync_engine(e):
            def rows(t, ap, s):
                e.dma_start(t[0:FULL, :], ap[0:FULL * RW].rearrange("(p j) -> p j", j=RW)).then_inc(s, 16)
                if REST:
                    e.dma_start(t[FULL:FULL + 1, 0:REST], ap[FULL * RW:E].rearrange("(a j) -> a j", a=1)).then_inc(s, 16)

            e.dma_start(ident[:], c_ident).then_inc(q["s_c"], 16)
            e.dma_start(xn[:, 0, :], x[0:P, :]).then_inc(q["s_x"], 16)
            e.dma_start(wt[:].rearrange("i l r o -> i (l r) o"), weights.rearrange("l r i o -> i (l r) o")).then_inc(q["s_w"], 16)
            e.dma_start(rt[:], roots.rearrange("l i o -> i l o")).then_inc(q["s_w"], 16)
            e.dma_start(bt[:], biases.rearrange("l o -> o l")).then_inc(q["s_w"], 16)
            e.wait_ge(q["s_fill"], 1)
            rows(a_dst, dst, q["s_e0"])
            e.dma_start(a_prev[0:1, 1:RW], dview[:, 0:RW - 1]).then_inc(q["s_e0"], 16)
            if FULL > 1:
                e.dma_start(a_prev[1:FULL, :], dst[RW - 1:FULL * RW - 1].rearrange("(p j) -> p j", j=RW)).then_inc(q["s_e0"], 16)
            if REST:
                e.dma_start(a_prev[FULL:FULL + 1, 0:REST], dview[:, FULL * RW - 1:E - 1]).then_inc(q["s_e0"], 16)
            e.dma_start(need_t[:], c_need).then_inc(q["s_e0"], 16)
            e.dma_start(valid[:], c_valid).then_inc(q["s_e0"], 16)
            rows(a_src, src, q["s_e0"])
            rows(a_typ, typ, q["s_e0"])
            nf = (N // P) - 1
            e.dma_start(xn[:, 1:1 + nf, :], x[P:P + nf * P, :].rearrange("(k p) f -> p k f", p=P)).then_inc(q["s_x"], 16)
            if bw[-1] < P:
                e.dma_start(xn[0:bw[-1], NB - 1, :], x[(NB - 1) * P:N, :]).then_inc(q["s_x"], 16)
            e.dma_start(iota[:], c_iota).then_inc(q["s_e1"], 16)
            n1 = FULL if REST else FULL - 1
            e.dma_start(a_next[0:n1, :], dst[1:1 + n1 * RW].rearrange("(p j) -> p j", j=RW)).then_inc(q["s_e1"], 16)
            last = E - 1 - n1 * RW
            if last:
                e.dma_start(a_next[n1:n1 + 1, 0:last], dview[:, n1 * RW + 1:E]).then_inc(q["s_e1"], 16)
            e.dma_start(lower[:], c_lower).then_inc(q["s_e1"], 16)
            e.dma_start(dumpc[:], c_col).then_inc(q["s_e1"], 16)
            for k in range(NB):
                store_y(e, 0, k)
            branch(e, "SP", sp_fast)

        n_rows = 1 + (REST > 0)
        N_E0 = 16 * (n_rows * 3 + 1 + (FULL > 1) + (REST > 0) + 2)
        n1_ = FULL if REST else FULL - 1
        N_E1 = 16 * (4 + (E - 1 - n1_ * RW > 0))
        N_X = 16 * (2 + (bw[-1] < P))

        def store_y(e, li, k):
            n = li * NB + k
            e.wait_ge(q["s_yev"], n + 1)
            e.dma_start(Y[li % 2][NR * P * k:NR * (P * k + bw[k]), :].rearrange("(n r) f -> n (r f)", r=NR),
                        yst[0:bw[k], n % YS, :]).then_inc(s_yd[n % YS], 16)

        def y_stored(e, li):
            for s in range(YS):
                e.wait_ge(s_yd[s], 16 * len(range(s, (li + 1) * NB, YS)))

        def out_batches():
            found = []
            for g in range(NG):
                ks = after[g]
                if ks:
                    found.append((g, ks))
            merged, run, at = [], [], None
            for g, ks in found:
                for k in ks:
                    run.append(k)
                    if len(run) == 4:
                        merged.append((g, run)); run = []
                if run and g == NG - 1:
                    merged.append((g, run)); run = []
            return merged

        batches = out_batches()
        batches_at = {}
        for n, (g, ks) in enumerate(batches):
            batches_at.setdefault(g, []).append((n, ks))

        def branch(e, name, fast):
            e.wait_ge(q["s_fl"], 1)
            v = e.value_load(flag_i[0:1, 0:1], min_val=0, max_val=4 * P)
            with e.If(v < 1):
                fast(e)
            with e.Else():
                general(e, name)

        def sp_fast(e):
            for li in (1, 2):
                for g in range(NG):
                    for k in after[g]:
                        store_y(e, li, k)
            for n, (g, ks) in enumerate(batches):
                e.wait_ge(q["s_no"], n + 1)
                full = [k for k in ks if bw[k] == P]
                o = zt[:, n % 2]
                cnt = 0
                if full:
                    e.dma_start(out[P * full[0]:P * (full[-1] + 1), :].rearrange("(k p) f -> p k f", p=P),
                                o[:, 0:len(full), :]).then_inc(s_od[n % 2], 16)
                if len(full) < len(ks):
                    k = ks[-1]
                    e.dma_start(out[P * k:N, :], o[0:bw[k], len(full), :]).then_inc(s_od[n % 2], 16)
            for s in range(2):
                e.wait_ge(s_od[s], stored(s, len(batches)))

        def stored(s, upto):
            total = 0
            for n, (g, ks) in enumerate(batches[:upto]):
                if n % 2 == s:
                    full = [k for k in ks if bw[k] == P]
                    total += 16 * ((len(full) > 0) + (len(full) < len(ks)))
            return total

        ring_total = [0] * R
        ring_need = {}
        for li in range(NL):
            for g in range(NG):
                n = li * NG + g
                ring_total[n % R] += 16 * len(tiles[g])
                ring_need[n] = ring_total[n % R]

        def gpsimd_engine(e):
            e.memset(a_dst[:], FAR)
            e.memset(a_next[:], FAR)
            e.memset(a_prev[:], -1)
            e.memset(a_src[:], 0)
            e.memset(a_typ[:], 0).then_inc(q["s_fill"], 1)
            e.wait_ge(q["s_tev"], 1)
            branch(e, "POOL", pool_fast)

        def pool_fast(e):
            for li in range(NL):
                y_stored(e, li)
                for g in range(NG):
                    n = li * NG + g
                    if n >= R:
                        e.wait_ge(q["s_pe"], n - R + 1)
                    for i, t in enumerate(tiles[g]):
                        m = rows_of[t]
                        at = (n % R) * 512 + i * P
                        e.indirect_dma_start(ring[0:m, at:at + P], None, Y[li % 2],
                                             bass.IndirectOffsetOnAxis(ap=idxc[0:m, t:t + 1], axis=0)
                                             ).then_inc(s_ring[n % R], 16)

        def pe_block(e, li, k):
            n = li * NB + k
            src_b, _ = node_src(li)
            h = src_b[:, P * k:P * k + bw[k]]
            e.wait_ge(q["s_xt"], n + 1)
            if n >= 2:
                e.wait_ge(q["s_yev"], n - 1)
                e.wait_ge(q["s_rev"], n - 1)
            e.matmul(psY[n % 2][0:bw[k], :], h, wt[:, li].rearrange("i r o -> i (r o)"),
                     start=True, stop=True).then_inc(q["s_ym"], 1)
            e.matmul(psR[n % 2][:, 0:bw[k]], rt[:, li, :], h, start=True, stop=True).then_inc(q["s_rm"], 1)

        def pe_cols(e, a, b0):
            for qd in range(8):
                last = e.transpose(psG[qd // 4][:, (qd % 4) * NP:(qd % 4 + 1) * NP], a[:, P * qd:P * (qd + 1)],
                                   ident[0:NP, 0:NP])
            last.then_inc(q["s_tp"], 1)

        def tensor_engine(e):
            def xt(k):
                if k == 0:
                    e.wait_ge(q["s_c"], 16)
                    e.wait_ge(q["s_x"], N_X)
                if k >= 2:
                    e.wait_ge(q["s_xt"], k - 1)
                e.transpose(psT[k % 2][:, 0:bw[k]], xn[0:bw[k], k, :], ident[0:bw[k], 0:bw[k]]).then_inc(q["s_st"], 1)

            xt(0)
            xt(1)
            e.wait_ge(q["s_w"], 48)
            for k in range(NB):
                pe_block(e, 0, k)
                if k + 2 < NB:
                    xt(k + 2)
                if k == min(8, NB - 1):
                    e.wait_ge(q["s_v"], 1)
                    e.matmul(psG[0][0:1, 0:1], chk[:, 4:5], ones[0:NP, 0:1], start=True, stop=True)
                    for h in range(2):
                        last = e.matmul(psG[1][0:1, h * NP:(h + 1) * NP], chk[:, 5 + h:6 + h],
                                        ident[0:NP, 0:NP], start=True, stop=True)
                    last.then_inc(q["s_tp"], 1)
                    for n, a in enumerate((a_idx, a_rel)):
                        e.wait_ge(q["s_tev" if n else "s_br"], 1)
                        e.wait_ge(q["s_v"], 2 + n)
                        pe_cols(e, a, n)
            e.wait_ge(q["s_tev"], 2)
            e.wait_ge(q["s_v"], 4)
            for d in range(2):
                for w in range(2):
                    last = e.transpose(psG[d][0:NR, w * NP:(w + 1) * NP], ends[:, d, w, :], ident[0:NP, 0:NP])
            last.then_inc(q["s_carry"], 1)
            e.wait_ge(q["s_v"], 5)
            for d in range(2):
                c = carry[:, d, 0:NP] if d == 0 else carry[:, d, 1:NP + 1]
                last = e.transpose(psG[d][0:NP, 256:256 + NR], c, ident[0:NR, 0:NR])
            last.then_inc(q["s_carry"], 1)
            e.wait_ge(q["s_v"], 6)
            pe_cols(e, a_w, 2)
            branch(e, "PE", pe_fast)

        def pe_fast(e):
            e.wait_ge(q["s_tev"], 3)
            for li in range(NL):
                for g in range(NG):
                    n = li * NG + g
                    e.wait_ge(q["s_S"], n + 1)
                    if n >= 2:
                        e.wait_ge(q["s_acc"], n - 1)
                    e.wait_ge(s_ring[n % R], ring_need[n])
                    for i, t in enumerate(tiles[g]):
                        m = rows_of[t]
                        at = (n % R) * 512 + i * P
                        last = e.matmul(psG[n % 2][:, 0:P], ring[0:m, at:at + P], S[0:m, n % NS, i, :],
                                        start=(i == 0), stop=(i == len(tiles[g]) - 1))
                    last.then_inc(q["s_pe"], 1)
                    if li < 2:
                        for k in after[g]:
                            pe_block(e, li + 1, k)
                    for b, ks in (batches_at.get(g, []) if li == 2 else []):
                        e.wait_ge(q["s_acc"], li * NG + g + 1)
                        if b >= 2:
                            e.wait_ge(q["s_va"], b - 1)
                        for j, k in enumerate(ks):
                            last = e.transpose(psT[b % 2][0:bw[k], j * D:(j + 1) * D],
                                               B[1][:, P * k:P * k + bw[k]], ident[:])
                        last.then_inc(q["s_fin"], 1)

        def act_out(e, li, k):
            n = li * NB + k
            _, dst_b = node_src(li)
            e.wait_ge(q["s_ym"], n + 1)
            if n >= YS:
                e.wait_ge(s_yd[n % YS], 16 * (n // YS))
            e.activation(yst[0:bw[k], n % YS, :], psY[n % 2][0:bw[k], :], ACT.Copy).then_inc(q["s_yev"], 1)
            e.wait_ge(q["s_rm"], n + 1)
            e.activation(dst_b[:, P * k:P * k + bw[k]], psR[n % 2][:, 0:bw[k]], ACT.Identity,
                         bias=bt[:, li:li + 1]).then_inc(q["s_rev"], 1)

        def scalar_engine(e):
            def cp(k):
                e.wait_ge(q["s_st"], k + 1)
                e.activation(B[0][:, P * k:P * k + bw[k]], psT[k % 2][:, 0:bw[k]], ACT.Copy).then_inc(q["s_xt"], 1)
            cp(0)
            for k in range(NB):
                if k + 1 < NB:
                    cp(k + 1)
                act_out(e, 0, k)
            branch(e, "ACT", act_fast)

        def act_fast(e):
            for li in range(2):
                for g in range(NG):
                    ks = after[g]
                    for i, k in enumerate(ks):
                        if i == 0:
                            e.wait_ge(q["s_acc"], li * NG + g + 1)
                        b = B[(li + 1) % 2][:, P * k:P * k + bw[k]]
                        e.activation(b, b, ACT.Relu).then_inc(q["s_xt"], 1)
                    for k in ks:
                        act_out(e, li + 1, k)
            for n, (g, ks) in enumerate(batches):
                e.wait_ge(q["s_sq"], n + 1)
                e.activation(sd[:, 0:len(ks)], mv[:, 0:len(ks), 1], ACT.Sqrt, bias=epst[:, 0:1]).then_inc(q["s_relu"], 1)

        def vector_engine(e):
            done = [0]

            def link(ins):
                done[0] += 1
                ins.then_inc(q["s_v2"], 1)
                e.wait_ge(q["s_v2"], done[0])

            e.memset(ones[:], 1.0)
            e.memset(epst[:], EPS)
            e.memset(carry[:], 0.0)
            e.memset(B[0][:, N:NW], 0.0)
            e.memset(B[1][:, N:NW], 0.0)
            e.wait_ge(q["s_e0"], N_E0)
            dv = a_dst[:].rearrange("p (h j) -> p h j", h=2)
            link(e.scalar_tensor_tensor(a_idx[:], a_src[:], float(NR), a_typ[:], ALU.mult, ALU.add))
            link(e.tensor_copy(chk[:, 5:7], dv[:, :, 0]))
            for h in range(2):
                o = 512 * h
                link(e.scalar_tensor_tensor(a_rel[:, o:o + 512], a_dst[:, o:o + 512], chk[:, 5 + h:6 + h],
                                            valid[:, o:o + 512], ALU.subtract, ALU.mult))
            link(e.tensor_reduce(chk[:, 0:1], a_rel[:], AX.X, ALU.max))
            link(e.tensor_tensor(same_n[:], a_prev[:], a_dst[:], ALU.subtract))
            link(e.tensor_reduce(chk[:, 1:2], same_n[:], AX.X, ALU.max))
            link(e.tensor_tensor(need_t[:], need_t[:], chk[:, 5:7], ALU.subtract))
            link(e.tensor_reduce(chk[:, 2:3], need_t[:], AX.X, ALU.max))
            link(e.tensor_scalar(chk[:, 0:1], chk[:, 0:1], float(P - 1), None, ALU.is_gt))
            link(e.tensor_scalar(chk[:, 1:3], chk[:, 1:3], 0.0, None, ALU.is_gt))
            link(e.tensor_reduce(chk[:, 4:5], chk[:, 0:3], AX.X, ALU.add))
            e.sem_inc(q["s_v"], 3)
            e.wait_ge(q["s_tp"], 1)
            e.tensor_copy(flag_i[:], psG[0][0:1, 0:1]).then_inc(q["s_fl"], 1)
            e.tensor_copy(brow[:].rearrange("a h p -> a (h p)"), psG[1][0:1, 0:2 * NP]).then_inc(q["s_br"], 1)

            def cols(c, nth):
                e.wait_ge(q["s_tp"], nth + 2)
                cv = c[:].rearrange("p (t q) -> p q t", q=8)
                for hh in range(2):
                    last = e.tensor_copy(cv[:, 4 * hh:4 * hh + 4, :],
                                         psG[hh][:, 0:4 * NP].rearrange("p (q t) -> p q t", q=4))
                last.then_inc(q["s_tev"], 1)

            cols(idxc, 0)
            cols(relc, 1)
            e.wait_ge(q["s_e1"], N_E1)
            link(e.tensor_tensor(same_p[:], a_dst[:], a_prev[:], ALU.is_equal))
            link(e.tensor_tensor(same_n[:], a_dst[:], a_next[:], ALU.is_equal))
            for r in range(NR):
                link(e.tensor_reduce(ends[:, 0, 0, r:r + 1], same_p[:], AX.X, ALU.min)) if r == 0 else None
                link(e.tensor_reduce(ends[:, 1, 0, r:r + 1], same_n[:], AX.X, ALU.min)) if r == 0 else None
                if r:
                    link(e.tensor_copy(ends[:, 0, 0, r:r + 1], ends[:, 0, 0, 0:1]))
                    link(e.tensor_copy(ends[:, 1, 0, r:r + 1], ends[:, 1, 0, 0:1]))
                link(e.tensor_scalar(mask[:], a_typ[:], float(r), None, ALU.is_equal))
                link(e.tensor_tensor_scan(fwd[:], same_p[:], mask[:], 0.0, ALU.mult, ALU.add))
                link(e.tensor_tensor_scan(bwd[:, ::-1], same_n[:, ::-1], mask[:, ::-1], 0.0, ALU.mult, ALU.add))
                link(e.tensor_copy(ends[:, 0, 1, r:r + 1], fwd[:, RW - 1:RW]))
                link(e.tensor_copy(ends[:, 1, 1, r:r + 1], bwd[:, 0:1]))
            e.sem_inc(q["s_v"], 1)
            e.wait_ge(q["s_carry"], 1)
            for d in range(2):
                for w in range(2):
                    link(e.tensor_copy(rowt[:, d, w, 0:NP], psG[d][0:NR, w * NP:(w + 1) * NP]))
            link(e.tensor_tensor_scan(carry[:, 0, 1:NP + 1], rowt[:, 0, 0, 0:NP], rowt[:, 0, 1, 0:NP], 0.0, ALU.mult, ALU.add))
            link(e.tensor_tensor_scan(carry[:, 1, 0:NP][:, ::-1], rowt[:, 1, 0, 0:NP][:, ::-1],
                                      rowt[:, 1, 1, 0:NP][:, ::-1], 0.0, ALU.mult, ALU.add))
            e.sem_inc(q["s_v"], 1)
            e.wait_ge(q["s_carry"], 2)
            for d in range(2):
                link(e.tensor_copy(cin[:, d, :], psG[d][0:NP, 256:256 + NR]))
            link(e.memset(a_w[:], 1.0))
            for r in range(NR):
                link(e.tensor_scalar(mask[:], a_typ[:], float(r), None, ALU.is_equal))
                link(e.tensor_tensor_scan(fwd[:], same_p[:], mask[:], cin[:, 0, r:r + 1], ALU.mult, ALU.add))
                link(e.tensor_tensor_scan(bwd[:, ::-1], same_n[:, ::-1], mask[:, ::-1], cin[:, 1, r:r + 1], ALU.mult, ALU.add))
                link(e.scalar_tensor_tensor(fwd[:], fwd[:], -1.0, bwd[:], ALU.add, ALU.add))
                link(e.copy_predicated(a_w[:], mask[:].bitcast(I32), fwd[:]))
            link(e.tensor_scalar(a_w[:], a_w[:], 1.0, None, ALU.max))
            link(e.reciprocal(a_w[:], a_w[:]))
            link(e.tensor_tensor(a_w[:], a_w[:], valid[:], ALU.mult))
            e.sem_inc(q["s_v"], 1)
            cols(wc, 2)
            branch(e, "DVE", dve_fast)

        def dve_fast(e):
            done = [0]

            def link(ins):
                done[0] += 1
                ins.then_inc(q["tDVE"], 1)
                e.wait_ge(q["tDVE"], done[0])

            e.wait_ge(q["s_tev"], 3)
            flat = [(li, g) for li in range(NL) for g in range(NG)]

            def build(n):
                li, g = flat[n]
                if n >= NS:
                    e.wait_ge(q["s_pe"], n - NS + 1)
                for i, t in enumerate(tiles[g]):
                    last = e.tensor_scalar(S[:, n % NS, i, :], iota[:], relc[:, t:t + 1], wc[:, t:t + 1],
                                           ALU.is_equal, ALU.mult)
                last.then_inc(q["s_S"], 1)

            def add(n):
                li, g = flat[n]
                _, b = node_src(li)
                v = e.value_load(base_ap[0:1, base_col(g):base_col(g) + 1], min_val=0, max_val=NW - P)
                if g == 0:
                    e.wait_ge(q["s_rev"], (li + 1) * NB)
                e.wait_ge(q["s_pe"], n + 1)
                if n:
                    e.wait_ge(q["s_acc"], n)
                w = b[:, bass.ds(v, P)]
                e.tensor_tensor(w, w, psG[n % 2][:, 0:P], ALU.add).then_inc(q["s_acc"], 1)

            def last_stage(n, ks):
                m = len(ks)
                r = bw[ks[-1]] if m == 1 else P
                z = zt[:, n % 2]
                e.wait_ge(q["s_fin"], n + 1)
                if n >= 2:
                    e.wait_ge(s_od[n % 2], stored(n % 2, n - 1))
                runs = [(0, m)] if bw[ks[-1]] == P else [(0, m - 1), (m - 1, m)]
                runs = [(a, b, bw[ks[b - 1]]) for a, b in runs if b > a]
                for a, b, rr in runs:
                    last = e.tensor_tensor(z[0:rr, a:b, :], psT[n % 2][0:rr, a * D:b * D].rearrange("p (k f) -> p k f", f=D),
                                           xn[0:rr, ks[a]:ks[a] + b - a, :], ALU.add)
                last.then_inc(q["s_va"], 1)
                e.wait_ge(q["s_va"], n + 1)
                if n:
                    e.wait_ge(q["s_relu"], n)
                for j in range(m):
                    rr = bw[ks[j]]
                    last = e.bn_stats(st[0:rr, j, :], z[0:rr, j, :])
                link(last)
                for j in range(m):
                    rr = bw[ks[j]]
                    last = e.bn_aggr(mv[0:rr, j, :], st[0:rr, j, :])
                last.then_inc(q["s_sq"], 1)

            def last_stage2(n, ks):
                m = len(ks)
                z = zt[:, n % 2]
                e.wait_ge(q["s_relu"], n + 1)
                link(e.reciprocal(rs[:, 0:m], sd[:, 0:m]))
                for j in range(m):
                    rr = bw[ks[j]]
                    last = e.tensor_scalar(z[0:rr, j, :], z[0:rr, j, :], mv[0:rr, j, 0:1], rs[0:rr, j:j + 1],
                                           ALU.subtract, ALU.mult)
                last.then_inc(q["s_no"], 1)

            link(e.memset(mv[:], 1.0))
            build(0)
            build(1)
            pending = []
            for n, (li, g) in enumerate(flat):
                if n + 2 < len(flat):
                    build(n + 2)
                add(n)
                if li == 2:
                    for b, ks in pending:
                        last_stage2(b, ks)
                    pending = []
                    here = batches_at.get(g, [])
                    for i, (b, ks) in enumerate(here):
                        if i:
                            last_stage2(*here[i - 1])
                        last_stage(b, ks)
                    pending = here[-1:]
            for b, ks in pending:
                last_stage2(b, ks)

        steps = []

        def step(who, fn, dma=False):
            steps.append((who, fn, dma))

        def loop(n, body):
            outer = list(steps)
            steps.clear()
            body()
            inner = list(steps)
            steps[:] = outer
            steps.append(("loop", n, inner))
            assert inner[0][0] == "DVE"
            step("DVE", lambda e, i: e.memset(g_junk[:], 0.0))

        g_idx, g_sidx = sb("g_idx", [P, 1], I32), sb("g_sidx", [P, 1], I32)
        g_key, g_pri, g_mul = sb("g_key", [P, 1]), sb("g_pri", [P, 1]), sb("g_mul", [P, 1])
        g_f, g_t, g_w = sb("g_f", [P, 1]), sb("g_t", [P, 1]), sb("g_w", [P, 1])
        g_junk = sb("g_junk", [1, 1])
        g_m, g_ml, g_kb = S[:, 0, 0, :], S[:, 0, 1, :], S[:, 0, 2, :]
        g_x, g_comb = S[:, 1, 0, :], S[:, 1, 1, :]
        keyc, dstc = relc, sb("dstc", [P, NT4])

        def dve(fn):
            step("DVE", fn)

        def to_tiles(a, c):
            for qd in range(8):
                step("PE", lambda e, i, qd=qd: e.transpose(psT[0][:, 0:NP], a[:, P * qd:P * (qd + 1)], ident[0:NP, 0:NP]))
                cv = c[:].rearrange("p (t q) -> p q t", q=8)
                dve(lambda e, i, qd=qd, cv=cv: e.tensor_copy(cv[:, qd, :], psT[0][:, 0:NP]))

        def equal_keys(limit, dump):
            dve(lambda e, i: e.tensor_scalar(g_kb, iota[:], 0.0, g_key[:, 0:1], ALU.mult, ALU.add))
            step("PE", lambda e, i: e.transpose(psT[1][:, 0:P], g_kb, ident[:]))
            dve(lambda e, i: e.tensor_scalar(g_m, psT[1][:, 0:P], g_key[:, 0:1], None, ALU.is_equal))
            dve(lambda e, i: e.tensor_tensor(g_ml, g_m, lower[:], ALU.mult))
            dve(lambda e, i: e.tensor_reduce(g_pri[:], g_ml, AX.X, ALU.add))
            dve(lambda e, i: e.tensor_scalar(g_f[:], g_pri[:], 0.0, None, ALU.is_equal))
            dve(lambda e, i: e.scalar_tensor_tensor(g_f[:], g_key[:], float(limit), g_f[:], ALU.is_lt, ALU.mult))
            dve(lambda e, i: e.scalar_tensor_tensor(g_t[:], g_key[:], dumpc[:, dump:dump + 1], g_f[:], ALU.subtract, ALU.mult))
            dve(lambda e, i: e.tensor_tensor(g_sidx[:], g_t[:], dumpc[:, dump:dump + 1], ALU.add))

        def count_tile():
            dve(lambda e, i: e.tensor_copy(g_key[:], keyc[:, bass.ds(i, 1)]))
            equal_keys(NK, 1)
            dve(lambda e, i: e.tensor_reduce(g_mul[:], g_m, AX.X, ALU.add))
            step("POOL", lambda e, i: e.indirect_dma_start(
                cnt_dram, bass.IndirectOffsetOnAxis(ap=g_sidx[:, 0:1], axis=0), g_mul[:], None,
                compute_op=ALU.add), True)

        def weigh_tile():
            dve(lambda e, i: e.tensor_copy(g_key[:], keyc[:, bass.ds(i, 1)]))
            dve(lambda e, i: e.tensor_scalar(g_idx[:], g_key[:], float(NK - 1), None, ALU.min))
            step("POOL", lambda e, i: e.indirect_dma_start(
                g_mul[:], None, cnt_dram, bass.IndirectOffsetOnAxis(ap=g_idx[:, 0:1], axis=0)), True)
            dve(lambda e, i: e.tensor_scalar(g_mul[:], g_mul[:], 1.0, None, ALU.max))
            dve(lambda e, i: e.reciprocal(g_mul[:], g_mul[:]))
            dve(lambda e, i: e.scalar_tensor_tensor(g_mul[:], g_key[:], float(NK), g_mul[:], ALU.is_lt, ALU.mult))
            dve(lambda e, i: e.tensor_copy(wc[:, bass.ds(i, 1)], g_mul[:]))

        def sum_tile(li):
            dve(lambda e, i: e.tensor_copy(g_idx[:], idxc[:, bass.ds(i, 1)]))
            dve(lambda e, i: e.tensor_copy(g_key[:], dstc[:, bass.ds(i, 1)]))
            dve(lambda e, i: e.tensor_copy(g_w[:], wc[:, bass.ds(i, 1)]))
            step("POOL", lambda e, i: e.indirect_dma_start(
                g_x, None, Y[li % 2], bass.IndirectOffsetOnAxis(ap=g_idx[:, 0:1], axis=0)), True)
            dve(lambda e, i: e.tensor_scalar(g_x, g_x, g_w[:, 0:1], None, ALU.mult))
            equal_keys(N, 0)
            step("PE", lambda e, i: e.matmul(psG[0][:, 0:P], g_m, g_x, start=True, stop=True))
            dve(lambda e, i: e.tensor_copy(g_comb, psG[0][:, 0:P]))
            step("POOL", lambda e, i: e.indirect_dma_start(
                acc_dram, bass.IndirectOffsetOnAxis(ap=g_sidx[:, 0:1], axis=0), g_comb, None,
                compute_op=ALU.add), True)

        def general_steps():
            acc3 = acc_dram.rearrange("(k p) f -> p k f", p=P)
            big = ring[:, 0:(NB + 1) * P]
            dve(lambda e, i: e.memset(ring[:], 0.0))
            step("SP", lambda e, i: e.dma_start(cnt_dram.rearrange("(p c) a -> p (c a)", p=P), ring[:, 0:NC]), True)
            dve(lambda e, i: e.tensor_copy(a_rel[:], a_dst[:]))
            to_tiles(a_rel, dstc)
            dve(lambda e, i: e.scalar_tensor_tensor(a_rel[:], a_dst[:], float(NR), a_typ[:], ALU.mult, ALU.add))
            to_tiles(a_rel, keyc)
            loop(NT, count_tile)
            loop(NT, weigh_tile)
            for li in range(NL):
                src_b, acc_b = node_src(li)
                dve(lambda e, i: e.memset(ring[:], 0.0))
                step("SP", lambda e, i: e.dma_start(acc3, big.rearrange("p (k f) -> p k f", f=D)), True)
                loop(NT, lambda: sum_tile(li))
                step("SP", lambda e, i: e.dma_start(big.rearrange("p (k f) -> p k f", f=D), acc3), True)
                for k in range(NB):
                    w = bw[k]
                    blk = acc_b[:, P * k:P * k + w]
                    oth = src_b[:, P * k:P * k + w]
                    step("PE", lambda e, i, k=k, w=w: e.transpose(psT[0][:, 0:w], ring[0:w, P * k:P * k + P], ident[0:w, 0:w]))
                    dve(lambda e, i, blk=blk, w=w: e.tensor_tensor(blk, blk, psT[0][:, 0:w], ALU.add))
                    if li < 2:
                        ln = li + 1
                        dve(lambda e, i, blk=blk: e.tensor_scalar(blk, blk, 0.0, None, ALU.max))
                        step("PE", lambda e, i, blk=blk, w=w, ln=ln: e.matmul(
                            psY[0][0:w, :], blk, wt[:, ln].rearrange("i r o -> i (r o)"), start=True, stop=True))
                        dve(lambda e, i, w=w: e.tensor_copy(yst[0:w, 0, :], psY[0][0:w, :]))
                        step("SP", lambda e, i, k=k, w=w, ln=ln: e.dma_start(
                            Y[ln % 2][NR * P * k:NR * (P * k + w), :].rearrange("(n r) f -> n (r f)", r=NR),
                            yst[0:w, 0, :]), True)
                        step("PE", lambda e, i, blk=blk, w=w, ln=ln: e.matmul(
                            psR[0][:, 0:w], rt[:, ln, :], blk, start=True, stop=True))
                        dve(lambda e, i, oth=oth, w=w, ln=ln: e.tensor_scalar(
                            oth, psR[0][:, 0:w], bt[:, ln:ln + 1], None, ALU.add))
                    else:
                        z = zt[0:w, 0, 0, :]
                        step("PE", lambda e, i, blk=blk, w=w: e.transpose(psT[0][0:w, 0:D], blk, ident[:]))
                        dve(lambda e, i, z=z, k=k, w=w: e.tensor_tensor(z, psT[0][0:w, 0:D], xn[0:w, k, :], ALU.add))
                        dve(lambda e, i, z=z, w=w: e.bn_stats(st[0:w, 0, :], z))
                        dve(lambda e, i, w=w: e.bn_aggr(mv[0:w, 0, :], st[0:w, 0, :]))
                        step("ACT", lambda e, i, w=w: e.activation(sd[0:w, 0:1], mv[0:w, 0, 1:2], ACT.Sqrt, bias=epst[0:w, 0:1]))
                        dve(lambda e, i, w=w: e.reciprocal(rs[0:w, 0:1], sd[0:w, 0:1]))
                        dve(lambda e, i, z=z, w=w: e.tensor_scalar(z, z, mv[0:w, 0, 0:1], rs[0:w, 0:1], ALU.subtract, ALU.mult))
                        step("SP", lambda e, i, z=z, k=k, w=w: e.dma_start(out[P * k:P * k + w, :], z), True)

        general_steps()

        def general(e, name):
            token = {n: q["t" + n] for n in ("SP", "PE", "ACT", "DVE", "POOL")}

            def emit(items, i, follows):
                for n, item in enumerate(items):
                    after_this = items[n + 1] if n + 1 < len(items) else follows
                    if item[0] == "loop":
                        first = item[2][0]
                        if any(s[0] == name for s in item[2]):
                            with e.Fori(0, item[1]) as j:
                                emit(item[2], j, first)
                        continue
                    who, fn, dma = item
                    if who != name:
                        continue
                    e.wait_ge(token[who], 1)
                    e.sem_clear(token[who])
                    to = after_this
                    while to is not None and to[0] == "loop":
                        to = to[2][0]
                    ins = fn(e, i)
                    if dma:
                        landed = q["gd" if name == "SP" else "gp"]
                        ins.then_inc(landed, 16)
                        e.wait_ge(landed, 16)
                        if name == "POOL":
                            e.dma_reset(range(landed.num, landed.num + 1))
                        e.sem_clear(landed)
                        if to is not None:
                            e.sem_inc(token[to[0]], 1)
                    elif to is not None:
                        ins.then_inc(token[to[0]], 1)

            if name == "DVE":
                e.wait_ge(q["s_tev"], 3)
                e.wait_ge(q["s_yev"], NB)
                e.wait_ge(q["s_rev"], NB)
                y_stored(e, 0)
                e.sem_inc(token["DVE"], 1)
            emit(steps, None, None)

        block.sync(sync_engine)
        block.gpsimd(gpsimd_engine)
        block.tensor(tensor_engine)
        block.scalar(scalar_engine)
        block.vector(vector_engine)
    return nc


_INS = ["x", "src", "dst", "edge_type_4", "L0_gnn_weights", "L0_gnn_roots", "L0_gnn_biases"]


def kernel(**inputs):
    import concourse.bacc as _bacc
    from concourse.bass_utils import run_bass_kernel_spmd as _run

    nc = _bacc.Bacc("TRN2", target_bir_lowering=False, num_devices=1)
    arrays, args = {}, []
    given = {n: np.ascontiguousarray(inputs[n]) for n in _INS}
    given.update(constants(given["x"].shape[0], given["src"].shape[0]))
    for name, a in given.items():
        arrays[f"in_{name}"] = a
        args.append(nc.dram_tensor(f"in_{name}", a.shape, mybir.dt.from_np(a.dtype), kind="ExternalInput").ap())
    o = nc.dram_tensor("out_0", given["x"].shape, F32, kind="ExternalOutput").ap()
    rgcn_kernel(nc, *args, o)
    r = _run(nc, [arrays], core_ids=[0])
    return r.results[0]["out_0"]
```

```python
import math

import numpy as np
import concourse.bass as bass
import concourse.mybir as mybir
from contextlib import ExitStack

F32 = mybir.dt.float32
I32 = mybir.dt.int32
U8 = mybir.dt.uint8
BF16 = mybir.dt.bfloat16
F16 = mybir.dt.float16
ALU = mybir.AluOpType
ACT = mybir.ActivationFunctionType
AX = mybir.AxisListType

P = 128
D = 128
NR = 4
NL = 3
RW = 1024
FAR = 1000000
EPS = 1e-5
WINDOWS = 8
SPAN = 116
CH = 7


class Plan:

    def __init__(self, N, E):
        self.N, self.E = N, E
        self.NP = NP = -(-E // RW)
        self.NG = NG = -(-E // 512)
        self.NT = -(-E // P)
        self.NB = NB = -(-N // P)
        node = lambda g: N * (g / NG) ** 2
        self.need = [max(0, int((node(g) - 96) // P)) for g in range(2 * NP)]
        self.win = []
        g = 0
        while len(self.win) < WINDOWS:
            h = g
            while h + 1 < NG // 2 and node(h + 1) - node(g) <= SPAN:
                h += 1
            if h == g:
                break
            m = (h - g) * 512 * P / N
            self.win.append((g, h, math.ceil((m + 5.5 * math.sqrt(m)) / P)))
            g = h
        self.G1 = g
        self.TH = 4 * g
        self.slot0, n = [], 0
        for _, _, c in self.win:
            self.slot0.append(n)
            n += c * NB
        self.NSL = n
        last = self.win[-1][0]
        self.KH = min(NB, max(int(node(last) + 40) // P + 2, int(node(g) + 40) // P + 1))
        self.most = np.full(2 * NP, 2.0 * FAR, np.float32)
        self.most[last] = P * (self.KH - 1)
        if g < NG:
            self.most[g] = min(self.most[g], P * self.KH - 1)
        self.chunks = [list(range(a, min(a + CH, NB))) for a in range(0, NB, CH)]
        self.phases, cur = [], []
        for w, (a, b, _) in enumerate(self.win):
            if cur and (b - self.win[cur[0]][0]) * 4 > 110:
                self.phases.append(cur)
                cur = []
            cur.append(w)
        self.phases.append(cur)
        self.SCW = max(4 * (self.win[p[-1]][1] - self.win[p[0]][0]) for p in self.phases)


def constants(N, E):
    pl = Plan(N, E)
    e = np.arange(P, dtype=np.float32)
    base, cap = [], []
    for w, (_, _, c) in enumerate(pl.win):
        for b in range(pl.NB):
            base.append((pl.slot0[w] + b * c) * P)
            cap.append(c * P)
    return {
        "c_ident": np.eye(P, dtype=np.float32),
        "c_iota": np.tile(e, (P, 1)),
        "c_tri": np.stack([(e[None, :] < e[:, None]), (e[:, None] < e[None, :])], 1).astype(np.float32),
        "c_col": np.stack([N + e, NR * N + e], 1).astype(np.float32),
        "c_valid": (np.arange(pl.NP * RW).reshape(pl.NP, RW) < E).astype(np.float32),
        "c_need": (P * np.array(pl.need, np.float32)).reshape(pl.NP, 2),
        "c_most": pl.most.reshape(pl.NP, 2),
        "c_iota16": np.tile(np.arange(NR * P, dtype=np.float16), (P, 1)),
        "c_bucket": np.tile(np.array([base, cap], np.float32)[None], (P, 1, 1)),
    }


def schedule(pl, R):
    gather, dense = 1.04, 0.64
    sparse = list(range(pl.G1, pl.NG))
    ntile = {g: min(4, pl.NT - 4 * g) for g in sparse}
    layers, pools = [], []
    for li in range(NL):
        pool, records = [], {}
        t = 65.0 if li == 0 else 0.0
        arrive, nxt, gap = {}, 0, R
        for n, g in enumerate(sparse):
            if li == 0 and nxt < len(pl.win) and n == gap:
                pool.append(("R", nxt))
                t += gather * 4 * (pl.win[nxt][1] - pl.win[nxt][0])
                records[nxt] = t + 6
                nxt, gap = nxt + 1, gap + 4
            pool.append(("S", n))
            t += gather * ntile[g]
            arrive[n] = t + 2
        while li == 0 and nxt < len(pl.win):
            pool.append(("R", nxt))
            t += gather * 4 * (pl.win[nxt][1] - pl.win[nxt][0])
            records[nxt] = t + 6
            nxt += 1
        pools.append(pool)

        todo = [(("X", b), 190.0 if li == 0 else 0.0, 1.0) for b in range(-(-pl.NB // 4))]
        for w, (_, _, c) in enumerate(pl.win):
            for k in range(len(pl.chunks)):
                each = dense + (0.25 + 0.25 * c if li == 0 else 0)
                todo.append((("C", w, k), records[w] if li == 0 else 0.0, each * len(pl.chunks[k])))
            todo.append((("F", w), 0.0, 2.0))
        items, at, done = [], 0.0, pl.KH
        late = list(range(pl.KH))
        if li < NL - 1:
            spill, eb = "E", 1.1
        else:
            spill, eb = "L", 0.3
        for what in pool:
            if what[0] == "R":
                items.append(what)
                continue
            n = what[1]
            g = sparse[n]
            ready = max(arrive[n], 190.0 if li == 0 else 0.0)
            while todo and (todo[0][0][0] != "C" or li > 0 or ("R", todo[0][0][1]) in items) \
                    and max(at, todo[0][1]) + todo[0][2] <= ready + 12:
                it, a, dur = todo.pop(0)
                at = max(at, a) + dur
                items.append(it)
            items.append(what)
            at = max(at, ready) + 0.22 * ntile[g]
            full = pl.NB if n == len(sparse) - 1 else min(pl.need[g + 1], pl.NB)
            early = ("X", -(-pl.NB // 4) - 1) in items
            if n == len(sparse) - 1 and not early:
                items += [x for x, _, _ in todo]
                todo, early = [], True
            if early:
                while done < full:
                    items.append((spill, done))
                    done += 1
                    at += eb
                if not todo and late and (full >= pl.KH):
                    items += [(spill, k) for k in late]
                    at += eb * len(late)
                    late = []
        items += [x for x, _, _ in todo]
        items += [(spill, k) for k in late]
        if li == NL - 1:
            merged, run, end = [], [], len(items)
            for n, it in enumerate(items):
                if it[0] != "L":
                    merged.append(it)
                    continue
                k = it[1]
                if run and k != run[-1] + 1:
                    merged.append(("L", tuple(run)))
                    run = []
                run.append(k)
                if len(run) == 4:
                    merged.append(("L", tuple(run)))
                    run = []
            if run:
                merged.append(("L", tuple(run)))
            items = merged
        layers.append(items)
    return layers, pools


def rgcn_kernel(nc, x, src, dst, typ, weights, roots, biases, c_ident, c_iota, c_tri, c_col, c_valid, c_need,
                c_most, c_iota16, c_bucket, out):
    N, E = x.shape[0], src.shape[0]
    pl = Plan(N, E)
    NP, NG, NT, NB, NSL, TH = pl.NP, pl.NG, pl.NT, pl.NB, pl.NSL, pl.TH
    NT4 = NP * 8
    NW = NB * P + P
    NK = NR * N
    R = 12
    NS = 3
    YS = 4
    NO = 3
    AS = 3
    NZ = 4
    FULL = E // RW
    REST = E - FULL * RW
    W = len(pl.win)
    NCH = len(pl.chunks)
    NX = -(-NB // 4)
    bw = [min(P, N - k * P) for k in range(NB)]
    sparse = list(range(pl.G1, NG))
    NSG = len(sparse)
    tiles = {g: [t for t in range(4 * g, 4 * g + 4) if t < NT] for g in range(NG)}
    rows_of = [min(P, E - t * P) for t in range(NT)]
    layers, pools = schedule(pl, R)

    acc_total = 0
    acc_at, acc_of, t_uses = {}, {}, []
    ta = tv = 0
    for k in range(NB):
        ta += 1
        t_uses.append(("s_tA", ta))
    t_of, lasts = {}, []
    for li, items in enumerate(layers):
        for n, it in enumerate(items):
            acc_at[li, n] = acc_total
            if it[0] in "SF":
                acc_total += 1
                acc_of[li, it] = acc_total
            elif it[0] == "C" and li == 0:
                for i in pl.chunks[it[2]]:
                    t_of[li, it, i] = len(t_uses)
                    ta += 1
                    t_uses.append(("s_tA", ta))
            elif it[0] == "X" and li > 0:
                t_of[li, it] = len(t_uses)
                t_uses.append(("s_xv", 2 * (li * NX + it[1]) + 1))
            elif it[0] == "L":
                t_of[li, it] = len(t_uses)
                tv += 1
                t_uses.append(("s_tV", tv))
                lasts.append(it[1])
    y_no = {(0, k): k for k in range(NB)}
    for li, items in enumerate(layers):
        for it in items:
            if it[0] == "E":
                y_no[li + 1, it[1]] = len(y_no)
    chunk_no = {}
    for li, items in enumerate(layers):
        for it in items:
            if it[0] == "C":
                chunk_no[li, it] = len(chunk_no)
    x_no = {(li, ("X", b)): li * NX + b for li in range(NL) for b in range(NX)}
    f_no = {(li, ("F", w)): li * W + w for li in range(NL) for w in range(W)}
    tile_no, v = {}, 0
    for it in layers[0]:
        if it[0] == "C":
            for i in pl.chunks[it[2]]:
                for c in range(pl.win[it[1]][2]):
                    tile_no[it, i, c] = v
                    v += 1

    ctx = ExitStack()
    with ctx:
        sb = lambda name, shape, dt=F32: ctx.enter_context(nc.sbuf_tensor(name, shape, dt))
        ps = lambda name, shape: ctx.enter_context(nc.psum_tensor(name, shape, F32))
        sem = lambda name: ctx.enter_context(nc.semaphore(name))
        ctx.enter_context(nc.allow_non_contiguous_dma("the biases, one element a partition"))

        Y = [nc.dram_tensor(f"ytab{i}", [NK, D], F32).ap() for i in range(2)]
        acc_dram = nc.dram_tensor("acc_dram", [(NB + 1) * P, D], F32).ap()
        NC = -(-(NK + P) // P)
        cnt_dram = nc.dram_tensor("cnt_dram", [NC * P, 1], F32).ap()
        cf_dram = nc.dram_tensor("cf_dram", [NP, 2 * NR], F32).ap()
        rec_dram = nc.dram_tensor("rec_dram", [NSL * P, 2], F32).ap()
        a_dram = [nc.dram_tensor(f"a_dram{w}", [P, NB * NR * P], F16).ap() for w in range(W)]

        ident, iota, tri = sb("ident", [P, P]), sb("iota", [P, P]), sb("tri", [P, 2, P])
        lower, upper = tri[:, 0, :], tri[:, 1, :]
        dumpc = sb("dumpc", [P, 2])
        iota16 = sb("iota16", [P, NR * P], F16)
        ones16 = sb("ones16", [P, P], F16)
        onesf = sb("onesf", [P, P])
        need_t, most_t = sb("need_t", [NP, 2]), sb("most_t", [NP, 2])
        ends = sb("ends", [NP, 2, 2, NR])
        carry = sb("carry", [NR, 2, NP + 2])
        cin = sb("cin", [NP, 2, NR])
        chk = sb("chk", [NP, 8])
        viol = sb("viol", [P, 4])
        basew = sb("basew", [P, W + 1])
        starts = [g for g, _, _ in pl.win] + [pl.G1]
        NF = starts[-1] // 2 + 1
        cfirst = sb("cfirst", [NP, 2, NR])
        cfb = sb("cfb", [P, NF, 2, NR])
        delta = sb("delta", [P, W])
        flag_i = sb("flag_i", [1, 1], I32)
        brow = sb("brow", [1, 2, NP], I32)
        idxc = sb("idxc", [P, NT4], I32)
        relc, wc, dstc = sb("relc", [P, NT4]), sb("wc", [P, NT4]), sb("dstc", [P, NT4])
        posc = sb("posc", [P, TH], I32)
        recv = sb("recv", [P, TH, 2])
        B = [sb("node0", [P, NW]), sb("node1", [P, NW])]
        wt = sb("wt", [P, NL, NR, D])
        rt = sb("rt", [P, NL, D])
        bt = sb("bt", [P, NL])
        ring = sb("ring", [P, max(R * 512, NB * P)])
        S = sb("S", [P, NS, 4, P])
        yst = sb("yst", [P, YS, NR * D])
        recs = sb("recs", [P, NSL, 2])
        V = sb("V", [P, max(4 * W * NB, 2 * NR * P + NO * (1 + NR) * P // 2)])
        bucket = V[:, 0:2 * W * NB].rearrange("p (a b) -> p a b", a=2)
        tot = V[:, 2 * W * NB:3 * W * NB].rearrange("p (w b) -> p w b", b=NB)
        offs = V[:, 3 * W * NB:4 * W * NB].rearrange("p (w b) -> p w b", b=NB)
        assert 3 * TH + 4 * (NP + 2) <= NS * 4 * P
        sv = S[:].rearrange("p s i c -> p (s i c)")
        blk, tmpi, relw = (sv[:, i * TH:(i + 1) * TH] for i in range(3))
        blk, tmpi = blk.bitcast(I32), tmpi.bitcast(I32)
        rowt = sv[0:NR, 3 * TH:3 * TH + 4 * (NP + 2)].rearrange("r (a b c) -> r a b c", a=2, b=2)
        ms, t1 = V[:, 0:NR * P], V[:, NR * P:2 * NR * P]
        oh = V[:, 2 * NR * P:2 * NR * P + NO * (1 + NR) * P // 2].bitcast(BF16).rearrange("p (v c) -> p v c", v=NO)
        ohs, ohk = oh[:, :, 0:P], oh[:, :, P:(1 + NR) * P]
        st = sb("st", [P, 4, 6])
        mv = sb("mv", [P, 4, 2])
        sd = sb("sd", [P, 4])
        rs = sb("rs", [P, 4])
        epst = sb("epst", [P, 1])
        xn = ring[:, 0:NB * P].rearrange("p (k f) -> p k f", f=D)
        zx = yst[:].rearrange("p s (j f) -> p s j f", f=D)

        scn = NB * pl.SCW
        early = 10 * RW + scn + 1 + -(-scn // 4)
        xw, aw, cw = 3 * NB * P // 2, AS * CH * NR * P // 2, max(W, 8) * NR * P
        U = sb("U", [P, max(early, xw + aw + cw)])
        row = lambda i, dt=F32: U[0:NP, i * RW:(i + 1) * RW].bitcast(dt)
        a_dst, a_typ, a_prev, a_next, a_src = (row(i, I32) for i in range(5))
        valid, a_idx, a_dstf, a_rel, a_w = (row(i) for i in range(5, 10))
        same_p, same_n, mask, fwd, bwd = row(2), row(3), row(4), row(6), row(7)
        sc = U[:, 10 * RW:10 * RW + scn + 1]
        m8 = U[:, 10 * RW + scn + 1:10 * RW + scn + 1 + -(-scn // 4)].bitcast(U8)
        xs = U[:, 0:xw].bitcast(BF16).rearrange("p (s k f) -> p s k f", s=3, f=D)
        aring = U[:, xw:xw + aw].bitcast(F16).rearrange("p (s i c) -> p s i c", s=AS, c=NR * P)
        cinv = U[:, xw + aw:xw + aw + cw].rearrange("p (w c) -> p w c", c=NR * P)

        psGR, psRB = ps("psGR", [P, 512]), ps("psRB", [P, 512])
        psG, psR = psGR[:, 0:P], psRB[:, 0:P]
        psY = [ps("psY0", [P, 512]), ps("psY1", [P, 512])]
        psT = [ps("psT0", [P, 512]), ps("psT1", [P, 512])]
        psD, psB = ps("psD", [P, 512]), ps("psB", [P, 512])
        psC = [psD, psB]

        names = ("s_e0 s_e1 s_e2 s_c s_x0 s_x1 s_w0 s_w1 s_fill s_v s_tp s_tev s_fl s_br s_small s_sm s_st s_xt "
                 "s_ym s_rm s_yev s_rev s_tA s_tV s_S s_pe s_acc s_fin s_sq s_sd s_no s_v2 s_v3 s_pos s_pf "
                 "s_rl s_bd s_oh s_dn s_fd s_fp s_xa s_xv s_xl s_dead tSP tPE tACT tDVE tPOOL gd gp s_cf s_rf").split()
        q = {n: sem(n) for n in names}
        s_ring = [sem(f"s_ring{i}") for i in range(R)]
        s_yd = [sem(f"s_yd{i}") for i in range(YS)]
        s_as = [sem(f"s_as{i}") for i in range(AS)]
        s_z = [sem(f"s_z{i}") for i in range(NZ)]
        s_sc = [sem(f"s_sc{w}") for w in range(W)]
        s_xs = [sem(f"s_xs{i}") for i in range(8)]
        block = ctx.enter_context(nc.Block())

        base_ap = brow[:].rearrange("a h p -> a (h p)")
        base_col = lambda g: (g % 2) * NP + g // 2
        dview = dst.rearrange("(a e) -> a e", a=1)
        nxt0 = min(7, NB - 2)

        def node_src(li):
            return B[li % 2], B[(li + 1) % 2]

        def t_free(e, u):
            if u >= 2:
                s, count = t_uses[u - 2]
                e.wait_ge(q[s], count)

        n_rows = 1 + (REST > 0)
        n1 = FULL if REST else FULL - 1
        last_n = E - 1 - n1 * RW
        N_E0 = 16 * 2 * n_rows
        N_E1 = 16 * (n_rows + 1 + (FULL > 1) + (REST > 0) + 8)
        N_E2 = 16 * (1 + (last_n > 0))

        def store_y(e, li, k):
            n = y_no[li, k]
            e.wait_ge(q["s_yev"], n + 1)
            e.dma_start(Y[li % 2][NR * P * k:NR * (P * k + bw[k]), :].rearrange("(n r) f -> n (r f)", r=NR),
                        yst[0:bw[k], n % YS, :]).then_inc(s_yd[n % YS], 16)

        def y_stored(e, li):
            for s in range(YS):
                e.wait_ge(s_yd[s], 16 * len(range(s, (li + 1) * NB, YS)))

        def a_view(w, k):
            ks = pl.chunks[k]
            return a_dram[w][:, ks[0] * NR * P:(ks[-1] + 1) * NR * P].rearrange("p (i c) -> p i c", c=NR * P)

        def load_rows(e, t, ap, s):
            e.dma_start(t[0:FULL, :], ap[0:FULL * RW].rearrange("(p j) -> p j", j=RW)).then_inc(s, 16)
            if REST:
                e.dma_start(t[FULL:FULL + 1, 0:REST], ap[FULL * RW:E].rearrange("(a j) -> a j", a=1)).then_inc(s, 16)

        def sync_engine(e):
            e.dma_start(ident[:], c_ident).then_inc(q["s_c"], 16)
            e.dma_start(xn[:, 0:nxt0, :], x[0:nxt0 * P, :].rearrange("(k p) f -> p k f", p=P)).then_inc(q["s_x0"], 16)
            e.dma_start(wt[:, 0], weights[0].rearrange("r i o -> i r o")).then_inc(q["s_w0"], 16)
            e.dma_start(rt[:, 0], roots[0]).then_inc(q["s_w0"], 16)
            e.dma_start(bt[:], biases.rearrange("l o -> o l")).then_inc(q["s_w0"], 16)
            e.wait_ge(q["s_fill"], 1)
            load_rows(e, a_src, src, q["s_e0"])
            load_rows(e, a_typ, typ, q["s_e0"])
            load_rows(e, a_dst, dst, q["s_e1"])
            nf = N // P
            e.dma_start(xn[:, nxt0:nf, :], x[nxt0 * P:nf * P, :].rearrange("(k p) f -> p k f", p=P)).then_inc(q["s_x1"], 16)
            if nf < NB:
                e.dma_start(xn[0:bw[-1], NB - 1, :], x[nf * P:N, :]).then_inc(q["s_x1"], 16)
            e.dma_start(a_prev[0:1, 1:RW], dview[:, 0:RW - 1]).then_inc(q["s_e1"], 16)
            if FULL > 1:
                e.dma_start(a_prev[1:FULL, :], dst[RW - 1:FULL * RW - 1].rearrange("(p j) -> p j", j=RW)).then_inc(q["s_e1"], 16)
            if REST:
                e.dma_start(a_prev[FULL:FULL + 1, 0:REST], dview[:, FULL * RW - 1:E - 1]).then_inc(q["s_e1"], 16)
            for t, c in ((need_t, c_need), (most_t, c_most), (valid, c_valid), (iota, c_iota), (tri, c_tri),
                         (dumpc, c_col), (iota16, c_iota16), (bucket, c_bucket)):
                e.dma_start(t if t is valid else t[:], c).then_inc(q["s_e1"], 16)
            e.dma_start(a_next[0:n1, :], dst[1:1 + n1 * RW].rearrange("(p j) -> p j", j=RW)).then_inc(q["s_e2"], 16)
            if last_n:
                e.dma_start(a_next[n1:n1 + 1, 0:last_n], dview[:, n1 * RW + 1:E]).then_inc(q["s_e2"], 16)
            e.dma_start(wt[:, 1:3].rearrange("i l r o -> i (l r) o"), weights[1:3].rearrange("l r i o -> i (l r) o")).then_inc(q["s_w1"], 16)
            e.dma_start(rt[:, 1:3], roots[1:3].rearrange("l i o -> i l o")).then_inc(q["s_w1"], 16)
            e.wait_ge(q["s_rf"], 1)
            e.dma_start(rec_dram.rearrange("(p c) a -> p (c a)", p=P), recs[:].rearrange("p c a -> p (c a)")).then_inc(q["s_pf"], 16)
            for k in range(NB):
                store_y(e, 0, k)
            branch(e, "SP", sp_fast)

        z_uses = {}

        def z_plan():
            total = [0] * NZ
            for b, ks in enumerate(lasts):
                parts = 1 if (bw[ks[-1]] == P or len(ks) == 1) else 2
                total[b % NZ] += 16 * parts
                load = total[b % NZ]
                total[b % NZ] += 16 * parts
                z_uses[b] = (load, total[b % NZ])
            return total

        z_total = z_plan()

        def z_parts(ks):
            full = [k for k in ks if bw[k] == P]
            parts = [(0, len(full), P)] if full else []
            if len(full) < len(ks):
                parts.append((len(full), len(ks), bw[ks[-1]]))
            return parts

        def node_rows(t, k0, m, rr):
            if rr == P:
                return t[P * k0:P * (k0 + m), :].rearrange("(k p) f -> p k f", p=P)
            return t[P * k0:P * k0 + rr, :].rearrange("(k p) f -> p k f", k=1)

        def sp_fast(e):
            def load_chunk(li, w, k):
                cc = chunk_no[li, ("C", w, k)]
                e.wait_ge(q["s_dn"], cc - AS + 1)
                e.wait_ge(s_as[cc % AS], 16 * (cc // AS))
                e.dma_start(aring[:, cc % AS, 0:len(pl.chunks[k]), :], a_view(w, k)).then_inc(s_as[cc % AS], 16)

            order = [(w, k) for w in range(W) for k in range(NCH)]
            e.wait_ge(q["s_tev"], 4)
            for li, items in enumerate(layers):
                if li:
                    if li == 1:
                        for s in range(AS):
                            e.wait_ge(s_as[s], 16 * len(range(s, W * NCH, AS)))
                    for w, k in order[0:2]:
                        load_chunk(li, w, k)
                zb = 0

                def z_load(b):
                    ks = lasts[b]
                    if b >= NZ:
                        e.wait_ge(s_z[b % NZ], z_uses[b - NZ][1])
                    for a, c, rr in z_parts(ks):
                        e.dma_start(zx[0:rr, b % NZ, a:c, :], node_rows(x, ks[a], c - a, rr)).then_inc(s_z[b % NZ], 16)

                if li == NL - 1:
                    y_stored(e, NL - 1)
                    for b in range(min(NZ - 1, len(lasts))):
                        z_load(b)
                for it in items:
                    if it[0] == "R":
                        w = it[1]
                        c = pl.win[w][2]
                        e.wait_ge(s_sc[w], 16 * 4 * (pl.win[w][1] - pl.win[w][0]))
                        lo = pl.slot0[w]
                        e.dma_start(recs[:, lo:lo + NB * c, :].rearrange("p (i c) a -> p i (c a)", c=c),
                                    rec_dram[lo * P:(lo + NB * c) * P, :].rearrange("(i p c) a -> p i (c a)", p=P, c=c)
                                    ).then_inc(q["s_rl"], 16)
                        e.wait_ge(q["s_rl"], 16 * (w + 1))
                    elif it[0] == "X" and li == 0:
                        b = it[1]
                        if b >= 8:
                            e.wait_ge(q["s_xv"], 2 * (b - 8) + 2)
                        ks = list(range(4 * b, min(4 * b + 4, NB)))
                        for a, c, rr in z_parts(ks):
                            e.dma_start(cinv[0:rr, b % 8, a * P:c * P].rearrange("p (k f) -> p k f", f=D),
                                        node_rows(x, ks[a], c - a, rr)).then_inc(s_xs[b % 8], 16)
                    elif it[0] == "C":
                        _, w, k = it
                        cc = chunk_no[li, it]
                        if li == 0:
                            i = pl.chunks[k][-1]
                            e.wait_ge(q["s_tA"], t_uses[t_of[li, it, i]][1])
                            e.dma_start(a_view(w, k), aring[:, cc % AS, 0:len(pl.chunks[k]), :]).then_inc(s_as[cc % AS], 16)
                        else:
                            at = w * NCH + k + 2
                            if at < len(order):
                                load_chunk(li, *order[at])
                    elif it[0] == "E":
                        store_y(e, li + 1, it[1])
                    elif it[0] == "L":
                        b = zb
                        zb += 1
                        e.wait_ge(q["s_no"], b + 1)
                        for a, c, rr in z_parts(it[1]):
                            e.dma_start(node_rows(out, it[1][a], c - a, rr), zx[0:rr, b % NZ, a:c, :]).then_inc(s_z[b % NZ], 16)
                        if b + NZ - 1 < len(lasts):
                            z_load(b + NZ - 1)
            for s in range(NZ):
                e.wait_ge(s_z[s], z_total[s])

        def branch(e, name, fast):
            e.wait_ge(q["s_fl"], 1)
            v = e.value_load(flag_i[0:1, 0:1], min_val=0, max_val=4 * P)
            with e.If(v < 1):
                fast(e)
            with e.Else():
                general(e, name)

        ring_total = [0] * R
        ring_need = {}
        for li in range(NL):
            for s in range(NSG):
                n = li * NSG + s
                ring_total[n % R] += 16 * len(tiles[sparse[s]])
                ring_need[n] = ring_total[n % R]
        AHEAD = min(R, NSG)

        def gather(e, li, s):
            n = li * NSG + s
            if n >= R:
                e.wait_ge(q["s_pe"], n - R + 1)
            for i, t in enumerate(tiles[sparse[s]]):
                m = rows_of[t]
                at = (n % R) * 512 + i * P
                e.indirect_dma_start(ring[0:m, at:at + P], None, Y[li % 2],
                                     bass.IndirectOffsetOnAxis(ap=idxc[0:m, t:t + 1], axis=0)
                                     ).then_inc(s_ring[n % R], 16)

        def gpsimd_engine(e):
            tail = FULL // 32 * 32
            e.memset(a_src[tail:NP, :], 0)
            e.memset(a_typ[tail:NP, :], 0)
            e.memset(a_dst[tail:NP, :], FAR)
            e.memset(a_next[tail:NP, :], FAR)
            last = e.memset(a_prev[tail:NP, :], -1)
            if tail:
                last = e.memset(a_prev[0:1, 0:1], -1)
            last.then_inc(q["s_fill"], 1)
            e.wait_ge(q["s_tev"], 1)
            y_stored(e, 0)
            for s in range(AHEAD):
                gather(e, 0, s)
            branch(e, "POOL", pool_fast)

        def pool_fast(e):
            for li in range(NL):
                if li:
                    y_stored(e, li)
                for kind, n in pools[li]:
                    if kind == "S":
                        if li or n >= AHEAD:
                            gather(e, li, n)
                        continue
                    a, b, _ = pl.win[n]
                    if n == 0:
                        e.wait_ge(q["s_pf"], 16)
                    ph = [i for i, p in enumerate(pl.phases) if n in p][0]
                    e.wait_ge(q["s_pos"], ph + 1)
                    for t in range(4 * a, 4 * b):
                        e.indirect_dma_start(rec_dram, bass.IndirectOffsetOnAxis(ap=posc[:, t:t + 1], axis=0),
                                             recv[:, t, :], None).then_inc(s_sc[n], 16)

        def pe_block(e, li, k):
            n = y_no[li, k]
            src_b, _ = node_src(li)
            h = src_b[:, P * k:P * k + bw[k]]
            if li == 0:
                e.wait_ge(q["s_tA"], n + 1)
            else:
                e.wait_ge(q["s_xt"], n - NB + 1)
            if n >= 2:
                e.wait_ge(q["s_yev"], n - 1)
            e.matmul(psY[n % 2][0:bw[k], :], h, wt[:, li].rearrange("i r o -> i (r o)"),
                     start=True, stop=True).then_inc(q["s_ym"], 1)
            e.wait_ge(q["s_rev"], n)
            e.matmul(psR[:, 0:bw[k]], rt[:, li, :], h, start=True, stop=True).then_inc(q["s_rm"], 1)

        def pe_cols(e, a):
            for qd in range(8):
                last = e.transpose(psC[qd // 4][:, (qd % 4) * NP:(qd % 4 + 1) * NP], a[:, P * qd:P * (qd + 1)],
                                   ident[0:NP, 0:NP])
            last.then_inc(q["s_tp"], 1)

        small = [0]

        def pe_small(e, *products):
            e.wait_ge(q["s_sm"], small[0])
            for o, a, b in products:
                last = e.matmul(o, a, b, start=True, stop=True)
            small[0] += 1
            last.then_inc(q["s_small"], 1)

        def pe_rank(e, i):
            if i == 0:
                e.wait_ge(q["s_v"], 4)
                pe_small(e, *[(psGR[:, 400 + w:401 + w], onesf[0:1, :], dstc[0:1, 4 * g:4 * g + 1])
                              for w, g in enumerate(starts)])
            w0, w1 = pl.phases[i][0], pl.phases[i][-1] + 1
            t = tot[:, w0:w1, :].rearrange("p w b -> p (w b)")
            e.wait_ge(q["s_v"], 5 + i)
            n = (w1 - w0) * NB
            pe_small(e, (psGR[:, 0:n], upper, t), (psGR[:, 200:200 + n], onesf[:], t))

        def tensor_engine(e):
            def xt(k):
                if k == 0:
                    e.wait_ge(q["s_c"], 16)
                    e.wait_ge(q["s_x0"], 16)
                if k == nxt0:
                    e.wait_ge(q["s_x1"], 16 * (1 + (N % P > 0)))
                t_free(e, k)
                e.transpose(psT[k % 2][:, 0:bw[k]], xn[0:bw[k], k, :], ident[0:bw[k], 0:bw[k]]).then_inc(q["s_st"], 1)

            xt(0)
            xt(1)
            e.wait_ge(q["s_w0"], 48)
            NPH = len(pl.phases)
            for k in range(NB):
                pe_block(e, 0, k)
                if k + 2 < NB:
                    xt(k + 2)
                if k == min(14, NB - 1):
                    for n, a in enumerate((a_idx, a_dstf)):
                        e.wait_ge(q["s_v"], 1 + n)
                        e.wait_ge(q["s_tev"], n)
                        pe_cols(e, a)
                if k == min(22, NB - 1):
                    e.wait_ge(q["s_v"], 3)
                    e.wait_ge(q["s_tev"], 2)
                    pe_cols(e, a_rel)
                if k == min(32, NB - 1):
                    pe_rank(e, 0)
            for i in range(1, NPH):
                pe_rank(e, i)
            e.wait_ge(q["s_v"], 5 + NPH)
            pe_small(e, (psGR[0:1, 410:411], viol[:, 3:4], onesf[:, 0:1]),
                     *[(psGR[0:1, h * NP:(h + 1) * NP], chk[:, 5 + h:6 + h], ident[0:NP, 0:NP]) for h in range(2)])
            e.wait_ge(q["s_tev"], 3)
            e.wait_ge(q["s_v"], 6 + NPH)
            for d in range(2):
                for w in range(2):
                    last = e.transpose(psC[d][0:NR, w * NP:(w + 1) * NP], ends[:, d, w, :], ident[0:NP, 0:NP])
            last.then_inc(q["s_tp"], 1)
            e.wait_ge(q["s_v"], 7 + NPH)
            for d in range(2):
                c = carry[:, d, 0:NP] if d == 0 else carry[:, d, 1:NP + 1]
                last = e.transpose(psC[d][0:NP, 256:256 + NR], c, ident[0:NR, 0:NR])
            last.then_inc(q["s_tp"], 1)
            e.wait_ge(q["s_v"], 8 + NPH)
            pe_cols(e, a_w)
            branch(e, "PE", pe_fast)

        def pe_fast(e):
            e.wait_ge(q["s_tev"], 4)
            e.wait_ge(q["s_sm"], 2 + len(pl.phases))
            e.wait_ge(q["s_w1"], 32)
            for li, items in enumerate(layers):
                src_b, acc_b = node_src(li)
                lb = 0
                for pos, it in enumerate(items):
                    if it[0] == "S":
                        n = li * NSG + it[1]
                        g = sparse[it[1]]
                        e.wait_ge(q["s_S"], n + 1)
                        e.wait_ge(q["s_acc"], acc_of[li, it] - 1)
                        e.wait_ge(s_ring[n % R], ring_need[n])
                        for i, t in enumerate(tiles[g]):
                            m = rows_of[t]
                            at = (n % R) * 512 + i * P
                            last = e.matmul(psG, ring[0:m, at:at + P], S[0:m, n % NS, i, :],
                                            start=(i == 0), stop=(i == len(tiles[g]) - 1))
                        last.then_inc(q["s_pe"], 1)
                    elif it[0] == "E":
                        pe_block(e, li + 1, it[1])
                    elif it[0] == "X" and li:
                        u = t_of[li, it]
                        t_free(e, u)
                        ks = range(4 * it[1], min(4 * it[1] + 4, NB))
                        e.wait_ge(q["s_xt"], li * NB)
                        for j, k in enumerate(ks):
                            last = e.transpose(psT[u % 2][0:bw[k], j * D:(j + 1) * D],
                                               src_b[:, P * k:P * k + bw[k]], ident[:])
                        last.then_inc(q["s_st"], 1)
                    elif it[0] == "C":
                        pe_chunk(e, li, it)
                    elif it[0] == "F":
                        f = f_no[li, it]
                        e.wait_ge(q["s_fd"], f + 1)
                        e.wait_ge(q["s_acc"], acc_of[li, it] - 1)
                        for r in range(NR):
                            last = e.matmul(psG, wt[:, li, r, :], ms[:, r * P:(r + 1) * P], start=(r == 0), stop=(r == NR - 1))
                        last.then_inc(q["s_fp"], 1)
                    elif it[0] == "L":
                        e.wait_ge(q["s_acc"], acc_at[li, pos])
                        u = t_of[li, it]
                        t_free(e, u)
                        for j, k in enumerate(it[1]):
                            last = e.transpose(psT[u % 2][0:bw[k], j * D:(j + 1) * D],
                                               acc_b[:, P * k:P * k + bw[k]], ident[:])
                        last.then_inc(q["s_fin"], 1)

        def pe_chunk(e, li, it):
            _, w, kc = it
            cc = chunk_no[li, it]
            slot = cc % AS
            ks = pl.chunks[kc]
            c = pl.win[w][2]
            f = f_no[li, ("F", w)]
            if kc == 0:
                e.wait_ge(q["s_fd"], f)
                e.wait_ge(q["s_xv"], 2 * NX * (li + 1))

            def dense(i):
                m = bw[i]
                a = aring[0:m, slot, i - ks[0], :]
                if li == 0:
                    e.wait_ge(q["s_tA"], t_uses[t_of[li, it, i]][1])
                    e.matmul(psB[:], ones16[0:m, :], a, start=(i == 0), stop=(i == NB - 1))
                for s in range(3):
                    last = e.matmul(psD[:], xs[0:m, s, i, :], a, start=(i == 0 and s == 0), stop=(i == NB - 1 and s == 2))
                if i == ks[-1]:
                    last.then_inc(q["s_dn"], 1)

            if li:
                e.wait_ge(s_as[slot], 16 * (cc // AS + 1))
            for i in ks:
                if li == 0:
                    u = t_of[li, it, i]
                    t_free(e, u)
                    for j in range(c):
                        v = tile_no[it, i, j]
                        e.wait_ge(q["s_oh"], v + 1)
                        e.matmul(psT[u % 2][:], ohs[:, v % NO, :], ohk[:, v % NO, :], start=(j == 0),
                                 stop=(j == c - 1)).then_inc(q["s_bd"], 1)
                    if i > ks[0]:
                        dense(i - 1)
                else:
                    dense(i)
            if li == 0:
                dense(ks[-1])

        def act_out(e, li, k):
            n = y_no[li, k]
            _, dst_b = node_src(li)
            e.wait_ge(q["s_ym"], n + 1)
            if n >= YS:
                e.wait_ge(s_yd[n % YS], 16 * (n // YS))
            e.activation(yst[0:bw[k], n % YS, :], psY[n % 2][0:bw[k], :], ACT.Copy).then_inc(q["s_yev"], 1)
            e.wait_ge(q["s_rm"], n + 1)
            e.activation(dst_b[:, P * k:P * k + bw[k]], psR[:, 0:bw[k]], ACT.Identity,
                         bias=bt[:, li:li + 1]).then_inc(q["s_rev"], 1)

        def scalar_engine(e):
            def cp(k):
                e.wait_ge(q["s_st"], k + 1)
                e.activation(B[0][:, P * k:P * k + bw[k]], psT[k % 2][:, 0:bw[k]], ACT.Copy).then_inc(q["s_tA"], 1)
            for k in range(NB):
                if k == 0:
                    cp(0)
                if k + 1 < NB:
                    cp(k + 1)
                act_out(e, 0, k)
            branch(e, "ACT", act_fast)

        def act_fast(e):
            e.wait_ge(q["s_v"], 8 + len(pl.phases))
            e.dma_start(cf_dram, cfirst[:].rearrange("p h r -> p (h r)")).then_inc(q["s_cf"], 16)
            e.wait_ge(q["s_cf"], 16)
            e.dma_start(cfb[:].rearrange("p g h r -> p (g h r)"),
                        cf_dram[0:NF, :].rearrange("(a g) c -> a (g c)", a=1).to_broadcast([P, NF * 2 * NR])
                        ).then_inc(q["s_cf"], 16)
            lb = 0
            for li, items in enumerate(layers):
                for pos, it in enumerate(items):
                    if it[0] == "E":
                        if items[pos - 1][0] == "E":
                            continue
                        run = []
                        while pos + len(run) < len(items) and items[pos + len(run)][0] == "E":
                            run.append(items[pos + len(run)][1])
                        e.wait_ge(q["s_acc"], acc_at[li, pos])
                        for j, k in enumerate(run):
                            b = B[(li + 1) % 2][:, P * k:P * k + bw[k]]
                            e.activation(b, b, ACT.Relu).then_inc(q["s_xt"], 1)
                            if j:
                                act_out(e, li + 1, run[j - 1])
                        act_out(e, li + 1, run[-1])
                    elif it[0] == "X":
                        b = it[1]
                        n = x_no[li, it]
                        for j, (a, c, rr, o, s_in, t_in) in enumerate(x_parts(e, li, it, "ACT")):
                            last = e.activation(o(0), s_in, ACT.Copy)
                        last.then_inc(q["s_xa"], 1)
                        e.wait_ge(q["s_xv"], 2 * n + 1)
                        for j, (a, c, rr, o, s_in, t_in) in enumerate(x_parts(e, li, it, None)):
                            last = e.activation(o(1), t_in, ACT.Copy)
                        last.then_inc(q["s_xa"], 1)
                    elif it[0] == "C" and li == 0:
                        _, w, kc = it
                        cc = chunk_no[li, it]
                        slot = cc % AS
                        c = pl.win[w][2]
                        if cc == 0:
                            e.wait_ge(q["s_tev"], 4)
                        if cc >= AS:
                            e.wait_ge(s_as[slot], 16 * (cc // AS))
                            e.wait_ge(q["s_dn"], cc - AS + 1)
                        for i in pl.chunks[kc]:
                            u = t_of[li, it, i]
                            e.wait_ge(q["s_bd"], tile_no[it, i, c - 1] + 1)
                            e.activation(aring[:, slot, i - pl.chunks[kc][0], :], psT[u % 2][:], ACT.Copy).then_inc(q["s_tA"], 1)
                    elif it[0] == "L":
                        m = len(it[1])
                        e.wait_ge(q["s_sq"], lb + 1)
                        e.activation(sd[:, 0:m], mv[:, 0:m, 1], ACT.Sqrt, bias=epst[:, 0:1]).then_inc(q["s_sd"], 1)
                        lb += 1

        def x_parts(e, li, it, who):
            b = it[1]
            ks = list(range(4 * b, min(4 * b + 4, NB)))
            if who:
                if li == 0:
                    parts = len(z_parts(ks))
                    before = sum(len(z_parts(list(range(4 * c, min(4 * c + 4, NB))))) for c in range(b % 8, b, 8))
                    e.wait_ge(q["s_tev"], 4)
                    e.wait_ge(s_xs[b % 8], 16 * (before + parts))
                else:
                    e.wait_ge(q["s_st"], NB + (li - 1) * NX + b + 1)
                    e.wait_ge(q["s_dn"], li * W * NCH)
            found = []
            for a, c, rr in z_parts(ks):
                if li == 0:
                    s_in = cinv[0:rr, b % 8, a * P:c * P]
                else:
                    s_in = psT[t_of[li, it] % 2][0:rr, a * P:c * P]
                found.append((a, c, rr, lambda s, a=a, c=c, rr=rr: xs[0:rr, s, ks[a]:ks[a] + c - a, :].rearrange("p k f -> p (k f)"),
                              s_in, t1[0:rr, a * P:c * P]))
            return found

        def vector_engine(e):
            done = [0]

            def link(ins):
                done[0] += 1
                ins.then_inc(q["s_v2"], 1)
                e.wait_ge(q["s_v2"], done[0])

            def ready():
                e.sem_inc(q["s_v"], 1)

            def cols(c, nth):
                e.wait_ge(q["s_tp"], nth + 1)
                cv = c[:].rearrange("p (t q) -> p q t", q=8)
                for hh in range(2):
                    last = e.tensor_copy(cv[:, 4 * hh:4 * hh + 4, :],
                                         psC[hh][:, 0:4 * NP].rearrange("p (q t) -> p q t", q=4))
                last.then_inc(q["s_tev"], 1)

            taken = [0]

            def small_there():
                taken[0] += 1
                e.wait_ge(q["s_small"], taken[0])

            e.memset(recs[:], -1.0).then_inc(q["s_rf"], 1)
            e.memset(onesf[:], 1.0)
            e.memset(ones16[:], 1.0)
            e.memset(epst[:], EPS)
            e.memset(carry[:], 0.0)
            e.memset(viol[:], 0.0)
            e.memset(mv[:], 1.0)
            e.memset(B[0][:, N:NW], 0.0)
            link(e.memset(B[1][:, N:NW], 0.0))
            e.wait_ge(q["s_e0"], N_E0)
            link(e.scalar_tensor_tensor(a_idx, a_src, float(NR), a_typ, ALU.mult, ALU.add))
            ready()
            e.wait_ge(q["s_e1"], N_E1)
            link(e.tensor_copy(a_dstf, a_dst))
            ready()
            dv = a_dst.rearrange("p (h j) -> p h j", h=2)
            link(e.tensor_copy(chk[:, 5:7], dv[:, :, 0]))
            for h in range(2):
                o = 512 * h
                link(e.scalar_tensor_tensor(a_rel[:, o:o + 512], a_dst[:, o:o + 512], chk[:, 5 + h:6 + h],
                                            valid[:, o:o + 512], ALU.subtract, ALU.mult))
            ready()
            cols(idxc, 0)
            cols(dstc, 1)
            e.wait_ge(q["s_tev"], 2)
            ready()
            link(e.tensor_scalar(blk[:], idxc[:, 0:TH], 9, None, ALU.arith_shift_right))
            onesb = onesf[:, 0:1]

            def rank(i):
                ws = pl.phases[i]
                c0, c1 = 4 * pl.win[ws[0]][0], 4 * pl.win[ws[-1]][1]
                n = c1 - c0
                m = m8[:, 0:NB * n]
                m3 = m.rearrange("p (b t) -> p b t", t=n)
                link(e.memset(sc[:, 0:1], 0.0))
                link(e.tensor_tensor(m3, blk[:, c0:c1].unsqueeze(1).to_broadcast([P, NB, n]),
                                     iota[:, 0:NB].unsqueeze(2).to_broadcast([P, NB, n]), ALU.is_equal))
                link(e.tensor_tensor_scan(sc[:, 1:1 + NB * n], onesb.to_broadcast([P, NB * n]), m, 0.0, ALU.mult, ALU.add))
                before = sc[:, 0:NB * n].rearrange("p (b t) -> p b t", t=n)
                behind = sc[:, 1:1 + NB * n].rearrange("p (b t) -> p b t", t=n)
                for w in ws:
                    a, b = 4 * pl.win[w][0] - c0, 4 * pl.win[w][1] - c0
                    link(e.tensor_tensor(tot[:, w, :], behind[:, :, b - 1], before[:, :, a], ALU.subtract))
                    link(e.tensor_tensor(offs[:, w, :], bucket[:, 0, w * NB:(w + 1) * NB], before[:, :, a], ALU.subtract))
                ready()
                if i == 0:
                    small_there()
                    e.tensor_copy(basew[:], psGR[:, 400:400 + W + 1]).then_inc(q["s_sm"], 1)
                small_there()
                w0, w1 = ws[0], ws[-1] + 1
                k = (w1 - w0) * NB
                o2 = offs[:, w0:w1, :].rearrange("p w b -> p (w b)")
                t2 = tot[:, w0:w1, :].rearrange("p w b -> p (w b)")
                link(e.tensor_tensor(o2, o2, psGR[:, 0:k], ALU.add))
                e.tensor_tensor(t2, psGR[:, 200:200 + k], bucket[:, 1, w0 * NB:w1 * NB], ALU.subtract).then_inc(q["s_sm"], 1)
                for w in ws:
                    a, b = 4 * pl.win[w][0] - c0, 4 * pl.win[w][1] - c0
                    link(e.tensor_tensor(before[:, :, a:b], before[:, :, a:b],
                                         offs[:, w, :].unsqueeze(2).to_broadcast([P, NB, b - a]), ALU.add))
                link(e.tensor_tensor(before, before, m3, ALU.mult))
                link(e.tensor_reduce(relw[:, c0:c1], sc[:, 0:NB * n].rearrange("p (b t) -> p t b", t=n), AX.X, ALU.add))
                link(e.tensor_copy(posc[:, c0:c1], relw[:, c0:c1]))
                if i == 0:
                    records()
                e.sem_inc(q["s_pos"], 1)

            def records():
                link(e.tensor_scalar(tmpi[:], idxc[:, 0:TH], 3, None, ALU.bitwise_and))
                link(e.tensor_copy(recv[:, :, 1], tmpi[:]))
                link(e.tensor_scalar(tmpi[:], idxc[:, 0:TH], 2, P - 1, ALU.arith_shift_right, ALU.bitwise_and))
                link(e.tensor_copy(recv[:, :, 0], tmpi[:]))
                e.wait_ge(q["s_sm"], 1)
                link(e.tensor_tensor(delta[:], basew[:, 1:W + 1], basew[:, 0:W], ALU.subtract))
                for w, (a, b, _) in enumerate(pl.win):
                    link(e.tensor_scalar(relw[:, 4 * a:4 * b], dstc[:, 4 * a:4 * b], basew[:, w:w + 1], None, ALU.subtract))
                link(e.scalar_tensor_tensor(recv[:, :, 1], recv[:, :, 1], float(P), relw[:], ALU.mult, ALU.add))
                link(e.tensor_reduce(viol[:, 1:2], relw[:], AX.X, ALU.max))
                link(e.tensor_scalar(viol[:, 1:2], viol[:, 1:2], float(P - 1), None, ALU.is_gt))

            rank(0)
            cols(relc, 2)
            for i in range(1, len(pl.phases)):
                rank(i)
            e.wait_ge(q["s_sm"], 1 + len(pl.phases))
            link(e.tensor_reduce(viol[:, 2:3], tot[:].rearrange("p w b -> p (w b)"), AX.X, ALU.max))
            link(e.tensor_scalar(viol[:, 2:3], viol[:, 2:3], 0.0, None, ALU.is_gt))
            link(e.tensor_reduce(chk[:, 0:1], a_rel, AX.X, ALU.max))
            link(e.tensor_tensor(fwd, a_prev, a_dst, ALU.subtract))
            link(e.tensor_reduce(chk[:, 1:2], fwd, AX.X, ALU.max))
            link(e.tensor_tensor(need_t[:], need_t[:], chk[:, 5:7], ALU.subtract))
            link(e.tensor_reduce(chk[:, 2:3], need_t[:], AX.X, ALU.max))
            link(e.tensor_tensor(most_t[:], chk[:, 5:7], most_t[:], ALU.subtract))
            link(e.tensor_reduce(chk[:, 3:4], most_t[:], AX.X, ALU.max))
            link(e.tensor_scalar(chk[:, 0:1], chk[:, 0:1], float(P - 1), None, ALU.is_gt))
            link(e.tensor_scalar(chk[:, 1:4], chk[:, 1:4], 0.0, None, ALU.is_gt))
            link(e.tensor_reduce(viol[0:NP, 0:1], chk[:, 0:4], AX.X, ALU.add))
            link(e.tensor_reduce(viol[:, 3:4], viol[:, 0:3], AX.X, ALU.add))
            ready()
            small_there()
            e.tensor_copy(flag_i[:], psGR[0:1, 410:411]).then_inc(q["s_fl"], 1)
            e.tensor_copy(brow[:].rearrange("a h p -> a (h p)"), psGR[0:1, 0:2 * NP]).then_inc(q["s_sm"], 1)

            e.wait_ge(q["s_e2"], N_E2)
            link(e.tensor_tensor(same_p, a_dst, a_prev, ALU.is_equal))
            link(e.tensor_tensor(same_n, a_dst, a_next, ALU.is_equal))
            for r in range(NR):
                if r == 0:
                    link(e.tensor_reduce(ends[:, 0, 0, 0:1], same_p, AX.X, ALU.min))
                    link(e.tensor_reduce(ends[:, 1, 0, 0:1], same_n, AX.X, ALU.min))
                else:
                    link(e.tensor_copy(ends[:, :, 0, r], ends[:, :, 0, 0]))
                link(e.tensor_scalar(mask, a_typ, float(r), None, ALU.is_equal))
                link(e.tensor_tensor_scan(fwd, same_p, mask, 0.0, ALU.mult, ALU.add))
                link(e.tensor_tensor_scan(bwd[:, ::-1], same_n[:, ::-1], mask[:, ::-1], 0.0, ALU.mult, ALU.add))
                link(e.tensor_copy(ends[:, 0, 1, r:r + 1], fwd[:, RW - 1:RW]))
                link(e.tensor_copy(ends[:, 1, 1, r:r + 1], bwd[:, 0:1]))
            ready()
            e.wait_ge(q["s_tp"], 4)
            for d in range(2):
                for w in range(2):
                    link(e.tensor_copy(rowt[:, d, w, 0:NP], psC[d][0:NR, w * NP:(w + 1) * NP]))
            link(e.tensor_tensor_scan(carry[:, 0, 1:NP + 1], rowt[:, 0, 0, 0:NP], rowt[:, 0, 1, 0:NP], 0.0, ALU.mult, ALU.add))
            link(e.tensor_tensor_scan(carry[:, 1, 0:NP][:, ::-1], rowt[:, 1, 0, 0:NP][:, ::-1],
                                      rowt[:, 1, 1, 0:NP][:, ::-1], 0.0, ALU.mult, ALU.add))
            ready()
            e.wait_ge(q["s_tp"], 5)
            for d in range(2):
                link(e.tensor_copy(cin[:, d, :], psC[d][0:NP, 256:256 + NR]))
            link(e.memset(a_w, 1.0))
            for r in range(NR):
                link(e.tensor_scalar(mask, a_typ, float(r), None, ALU.is_equal))
                link(e.tensor_tensor_scan(fwd, same_p, mask, cin[:, 0, r:r + 1], ALU.mult, ALU.add))
                link(e.tensor_tensor_scan(bwd[:, ::-1], same_n[:, ::-1], mask[:, ::-1], cin[:, 1, r:r + 1], ALU.mult, ALU.add))
                link(e.scalar_tensor_tensor(fwd, fwd, -1.0, bwd, ALU.add, ALU.add))
                firsts = [v.rearrange("p (h j) -> p h j", h=2)[:, :, 0] for v in (fwd, mask)]
                e.scalar_tensor_tensor(cfirst[:, :, r], firsts[0], 1.0, firsts[1], ALU.add, ALU.subtract)
                link(e.copy_predicated(a_w, mask.bitcast(I32), fwd))
            link(e.tensor_scalar(a_w, a_w, 1.0, None, ALU.max))
            link(e.reciprocal(a_w, a_w))
            link(e.tensor_tensor(a_w, a_w, valid, ALU.mult))
            ready()
            cols(wc, 5)
            e.wait_ge(q["s_tev"], 4)
            branch(e, "DVE", dve_fast)

        def dve_fast(e):
            done = [0]

            def link(ins):
                done[0] += 1
                ins.then_inc(q["s_v3"], 1)
                e.wait_ge(q["s_v3"], done[0])

            NN = NL * NSG

            def build(n):
                g = sparse[n % NSG]
                if n >= NS:
                    e.wait_ge(q["s_pe"], n - NS + 1)
                for i, t in enumerate(tiles[g]):
                    last = e.tensor_scalar(S[:, n % NS, i, :], iota[:], relc[:, t:t + 1], wc[:, t:t + 1],
                                           ALU.is_equal, ALU.mult)
                last.then_inc(q["s_S"], 1)

            def add(li, it, g, part, s_part, count):
                _, b = node_src(li)
                v = e.value_load(base_ap[0:1, base_col(g):base_col(g) + 1], min_val=0, max_val=NW - P)
                n = acc_of[li, it]
                e.wait_ge(q["s_rev"], (li + 1) * NB)
                e.wait_ge(q[s_part], count)
                if n > 1:
                    e.wait_ge(q["s_acc"], n - 1)
                w = b[:, bass.ds(v, P)]
                e.tensor_tensor(w, w, part, ALU.add).then_inc(q["s_acc"], 1)

            def onehots(it):
                _, w, kc = it
                c = pl.win[w][2]
                if kc == 0:
                    e.wait_ge(q["s_rl"], 16 * (w + 1))
                for i in pl.chunks[kc]:
                    for j in range(c):
                        v = tile_no[it, i, j]
                        if v >= NO:
                            e.wait_ge(q["s_bd"], v - NO + 1)
                        at = pl.slot0[w] + i * c + j
                        e.tensor_scalar(ohs[:, v % NO, :], iota16[:, 0:P], recs[:, at, 0:1], None, ALU.is_equal)
                        e.tensor_scalar(ohk[:, v % NO, :], iota16[:], recs[:, at, 1:2], None, ALU.is_equal).then_inc(q["s_oh"], 1)

            def last_stage(b, it):
                ks = it[1]
                z = zx[:, b % NZ]
                u = t_of[NL - 1, it]
                e.wait_ge(q["s_fin"], b + 1)
                e.wait_ge(s_z[b % NZ], z_uses[b][0])
                for a, c, rr in z_parts(ks):
                    last = e.tensor_tensor(z[0:rr, a:c, :], psT[u % 2][0:rr, a * D:c * D].rearrange("p (k f) -> p k f", f=D),
                                           z[0:rr, a:c, :], ALU.add)
                last.then_inc(q["s_tV"], 1)
                e.wait_ge(q["s_tV"], t_uses[u][1])
                if b:
                    e.wait_ge(q["s_sd"], b)
                for j, k in enumerate(ks):
                    last = e.bn_stats(st[0:bw[k], j, :], z[0:bw[k], j, :])
                link(last)
                for j, k in enumerate(ks):
                    last = e.bn_aggr(mv[0:bw[k], j, :], st[0:bw[k], j, :])
                last.then_inc(q["s_sq"], 1)

            def last_stage2(b, it):
                ks = it[1]
                z = zx[:, b % NZ]
                e.wait_ge(q["s_sd"], b + 1)
                link(e.reciprocal(rs[:, 0:len(ks)], sd[:, 0:len(ks)]))
                for j, k in enumerate(ks):
                    rr = bw[k]
                    last = e.tensor_scalar(z[0:rr, j, :], z[0:rr, j, :], mv[0:rr, j, 0:1], rs[0:rr, j:j + 1],
                                           ALU.subtract, ALU.mult)
                last.then_inc(q["s_no"], 1)

            build(0)
            build(1)
            lb, pending = 0, None
            for li, items in enumerate(layers):
                for pos, it in enumerate(items):
                    if pending and it[0] != "C":
                        last_stage2(*pending)
                        pending = None
                    if it[0] == "S":
                        n = li * NSG + it[1]
                        if n + 2 < NN:
                            build(n + 2)
                        add(li, it, sparse[it[1]], psG, "s_pe", n + 1)
                    elif it[0] == "C" and li == 0:
                        onehots(it)
                    elif it[0] == "X":
                        n = x_no[li, it]
                        parts = x_parts(e, li, it, "DVE")
                        e.wait_ge(q["s_xa"], 2 * n + 1)
                        e.wait_ge(q["s_xv"], 2 * n)
                        for a, c, rr, o, s_in, t_in in parts:
                            last = e.tensor_tensor(t_in, s_in, o(0), ALU.subtract)
                        last.then_inc(q["s_xv"], 1)
                        e.wait_ge(q["s_xa"], 2 * n + 2)
                        for a, c, rr, o, s_in, t_in in parts:
                            last = e.tensor_tensor(o(2), t_in, o(1), ALU.subtract)
                        last.then_inc(q["s_xv"], 1)
                    elif it[0] == "F":
                        w = it[1]
                        f = f_no[li, it]
                        e.wait_ge(q["s_dn"], chunk_no[li, ("C", w, NCH - 1)] + 1)
                        if li == 0:
                            e.wait_ge(q["s_cf"], 32)
                            cv = cinv[:, w, :].rearrange("p (r d) -> p r d", r=NR)
                            for r in range(NR):
                                g = starts[w + 1]
                                last = e.tensor_scalar(cv[:, r, :], iota[:], delta[:, w:w + 1],
                                                       cfb[:, g // 2, g % 2, r:r + 1], ALU.is_equal, ALU.mult)
                            link(last)
                            g = starts[w]
                            link(e.tensor_tensor(cv[:, :, 0], cv[:, :, 0], cfb[:, g // 2, g % 2, :], ALU.max))
                            link(e.scalar_tensor_tensor(cinv[:, w, :], psB[:], 1.0, cinv[:, w, :], ALU.max, ALU.max))
                            link(e.reciprocal(cinv[:, w, :], cinv[:, w, :]))
                        if f:
                            e.wait_ge(q["s_fp"], f)
                        e.tensor_tensor(ms[:], psD[:], cinv[:, w, :], ALU.mult).then_inc(q["s_fd"], 1)
                        add(li, it, pl.win[w][0], psG, "s_fp", f + 1)
                    elif it[0] == "L":
                        last_stage(lb, it)
                        pending = (lb, it)
                        lb += 1
            if pending:
                last_stage2(*pending)

        steps = []

        def step(who, fn, dma=False):
            steps.append((who, fn, dma))

        def loop(n, body):
            outer = list(steps)
            steps.clear()
            body()
            inner = list(steps)
            steps[:] = outer
            steps.append(("loop", n, inner))
            assert inner[0][0] == "DVE"
            step("DVE", lambda e, i: e.memset(g_junk[:], 0.0))

        g_idx, g_sidx = sb("g_idx", [P, 1], I32), sb("g_sidx", [P, 1], I32)
        g_key, g_pri, g_mul = sb("g_key", [P, 1]), sb("g_pri", [P, 1]), sb("g_mul", [P, 1])
        g_f, g_t, g_w = sb("g_f", [P, 1]), sb("g_t", [P, 1]), sb("g_w", [P, 1])
        g_junk = sb("g_junk", [1, 1])
        g_m, g_ml, g_kb = S[:, 0, 0, :], S[:, 0, 1, :], S[:, 0, 2, :]
        g_x, g_comb = S[:, 1, 0, :], S[:, 1, 1, :]
        keyc = relc

        def dve(fn):
            step("DVE", fn)

        def equal_keys(limit, dump):
            dve(lambda e, i: e.tensor_scalar(g_kb, iota[:], 0.0, g_key[:, 0:1], ALU.mult, ALU.add))
            step("PE", lambda e, i: e.transpose(psT[1][:, 0:P], g_kb, ident[:]))
            dve(lambda e, i: e.tensor_scalar(g_m, psT[1][:, 0:P], g_key[:, 0:1], None, ALU.is_equal))
            dve(lambda e, i: e.tensor_tensor(g_ml, g_m, lower[:], ALU.mult))
            dve(lambda e, i: e.tensor_reduce(g_pri[:], g_ml, AX.X, ALU.add))
            dve(lambda e, i: e.tensor_scalar(g_f[:], g_pri[:], 0.0, None, ALU.is_equal))
            dve(lambda e, i: e.scalar_tensor_tensor(g_f[:], g_key[:], float(limit), g_f[:], ALU.is_lt, ALU.mult))
            dve(lambda e, i: e.scalar_tensor_tensor(g_t[:], g_key[:], dumpc[:, dump:dump + 1], g_f[:], ALU.subtract, ALU.mult))
            dve(lambda e, i: e.tensor_tensor(g_sidx[:], g_t[:], dumpc[:, dump:dump + 1], ALU.add))

        def count_tile():
            dve(lambda e, i: e.tensor_copy(g_key[:], keyc[:, bass.ds(i, 1)]))
            equal_keys(NK, 1)
            dve(lambda e, i: e.tensor_reduce(g_mul[:], g_m, AX.X, ALU.add))
            step("POOL", lambda e, i: e.indirect_dma_start(
                cnt_dram, bass.IndirectOffsetOnAxis(ap=g_sidx[:, 0:1], axis=0), g_mul[:], None,
                compute_op=ALU.add), True)

        def weigh_tile():
            dve(lambda e, i: e.tensor_copy(g_key[:], keyc[:, bass.ds(i, 1)]))
            dve(lambda e, i: e.tensor_scalar(g_idx[:], g_key[:], float(NK - 1), None, ALU.min))
            step("POOL", lambda e, i: e.indirect_dma_start(
                g_mul[:], None, cnt_dram, bass.IndirectOffsetOnAxis(ap=g_idx[:, 0:1], axis=0)), True)
            dve(lambda e, i: e.tensor_scalar(g_mul[:], g_mul[:], 1.0, None, ALU.max))
            dve(lambda e, i: e.reciprocal(g_mul[:], g_mul[:]))
            dve(lambda e, i: e.scalar_tensor_tensor(g_mul[:], g_key[:], float(NK), g_mul[:], ALU.is_lt, ALU.mult))
            dve(lambda e, i: e.tensor_copy(wc[:, bass.ds(i, 1)], g_mul[:]))

        def sum_tile(li):
            dve(lambda e, i: e.tensor_copy(g_idx[:], idxc[:, bass.ds(i, 1)]))
            dve(lambda e, i: e.tensor_copy(g_key[:], dstc[:, bass.ds(i, 1)]))
            dve(lambda e, i: e.tensor_copy(g_w[:], wc[:, bass.ds(i, 1)]))
            step("POOL", lambda e, i: e.indirect_dma_start(
                g_x, None, Y[li % 2], bass.IndirectOffsetOnAxis(ap=g_idx[:, 0:1], axis=0)), True)
            dve(lambda e, i: e.tensor_scalar(g_x, g_x, g_w[:, 0:1], None, ALU.mult))
            equal_keys(N, 0)
            step("PE", lambda e, i: e.matmul(psG, g_m, g_x, start=True, stop=True))
            dve(lambda e, i: e.tensor_copy(g_comb, psG))
            step("POOL", lambda e, i: e.indirect_dma_start(
                acc_dram, bass.IndirectOffsetOnAxis(ap=g_sidx[:, 0:1], axis=0), g_comb, None,
                compute_op=ALU.add), True)

        def general_steps():
            acc3 = acc_dram.rearrange("(k p) f -> p k f", p=P)
            big = ring[:, 0:NB * P].rearrange("p (k f) -> p k f", f=D)
            dve(lambda e, i: e.memset(ring[:], 0.0))
            step("SP", lambda e, i: e.dma_start(cnt_dram.rearrange("(p c) a -> p (c a)", p=P), ring[:, 0:NC]), True)
            dve(lambda e, i: e.tensor_scalar(U[:, 0:NT4].bitcast(I32), idxc[:], NR - 1, None, ALU.bitwise_and))
            dve(lambda e, i: e.scalar_tensor_tensor(keyc[:], dstc[:], float(NR), U[:, 0:NT4].bitcast(I32), ALU.mult, ALU.add))
            loop(NT, count_tile)
            loop(NT, weigh_tile)
            for li in range(NL):
                src_b, acc_b = node_src(li)
                dve(lambda e, i: e.memset(ring[:], 0.0))
                step("SP", lambda e, i: e.dma_start(acc3[:, 0:NB, :], big), True)
                step("SP", lambda e, i: e.dma_start(acc3[:, NB:NB + 1, :], big[:, 0:1, :]), True)
                loop(NT, lambda: sum_tile(li))
                step("SP", lambda e, i: e.dma_start(big, acc3[:, 0:NB, :]), True)
                for k in range(NB):
                    w = bw[k]
                    blk = acc_b[:, P * k:P * k + w]
                    oth = src_b[:, P * k:P * k + w]
                    step("PE", lambda e, i, k=k, w=w: e.transpose(psT[0][:, 0:w], ring[0:w, P * k:P * k + P], ident[0:w, 0:w]))
                    dve(lambda e, i, blk=blk, w=w: e.tensor_tensor(blk, blk, psT[0][:, 0:w], ALU.add))
                    if li < 2:
                        ln = li + 1
                        dve(lambda e, i, blk=blk: e.tensor_scalar(blk, blk, 0.0, None, ALU.max))
                        step("PE", lambda e, i, blk=blk, w=w, ln=ln: e.matmul(
                            psY[0][0:w, :], blk, wt[:, ln].rearrange("i r o -> i (r o)"), start=True, stop=True))
                        dve(lambda e, i, w=w: e.tensor_copy(yst[0:w, 0, :], psY[0][0:w, :]))
                        step("SP", lambda e, i, k=k, w=w, ln=ln: e.dma_start(
                            Y[ln % 2][NR * P * k:NR * (P * k + w), :].rearrange("(n r) f -> n (r f)", r=NR),
                            yst[0:w, 0, :]), True)
                        step("PE", lambda e, i, blk=blk, w=w, ln=ln: e.matmul(
                            psR[:, 0:w], rt[:, ln, :], blk, start=True, stop=True))
                        dve(lambda e, i, oth=oth, w=w, ln=ln: e.tensor_scalar(
                            oth, psR[:, 0:w], bt[:, ln:ln + 1], None, ALU.add))
                    else:
                        z = zx[0:w, 0, 0, :]
                        step("SP", lambda e, i, z=z, k=k, w=w: e.dma_start(z, x[P * k:P * k + w, :]), True)
                        step("PE", lambda e, i, blk=blk, w=w: e.transpose(psT[0][0:w, 0:D], blk, ident[:]))
                        dve(lambda e, i, z=z, k=k, w=w: e.tensor_tensor(z, psT[0][0:w, 0:D], z, ALU.add))
                        dve(lambda e, i, z=z, w=w: e.bn_stats(st[0:w, 0, :], z))
                        dve(lambda e, i, w=w: e.bn_aggr(mv[0:w, 0, :], st[0:w, 0, :]))
                        step("ACT", lambda e, i, w=w: e.activation(sd[0:w, 0:1], mv[0:w, 0, 1:2], ACT.Sqrt, bias=epst[0:w, 0:1]))
                        dve(lambda e, i, w=w: e.reciprocal(rs[0:w, 0:1], sd[0:w, 0:1]))
                        dve(lambda e, i, z=z, w=w: e.tensor_scalar(z, z, mv[0:w, 0, 0:1], rs[0:w, 0:1], ALU.subtract, ALU.mult))
                        step("SP", lambda e, i, z=z, k=k, w=w: e.dma_start(out[P * k:P * k + w, :], z), True)

        general_steps()

        def general(e, name):
            token = {n: q["t" + n] for n in ("SP", "PE", "ACT", "DVE", "POOL")}

            def emit(items, i, follows):
                for n, item in enumerate(items):
                    after_this = items[n + 1] if n + 1 < len(items) else follows
                    if item[0] == "loop":
                        first = item[2][0]
                        if any(s[0] == name for s in item[2]):
                            with e.Fori(0, item[1]) as j:
                                emit(item[2], j, first)
                        continue
                    who, fn, dma = item
                    if who != name:
                        continue
                    e.wait_ge(token[who], 1)
                    e.sem_clear(token[who])
                    to = after_this
                    while to is not None and to[0] == "loop":
                        to = to[2][0]
                    ins = fn(e, i)
                    if dma:
                        landed = q["gd" if name == "SP" else "gp"]
                        ins.then_inc(landed, 16)
                        e.wait_ge(landed, 16)
                        if name == "POOL":
                            e.dma_reset(range(landed.num, landed.num + 1))
                        e.sem_clear(landed)
                        if to is not None:
                            e.sem_inc(token[to[0]], 1)
                    elif to is not None:
                        ins.then_inc(token[to[0]], 1)

            if name == "DVE":
                e.wait_ge(q["s_tev"], 4)
                e.wait_ge(q["s_pf"], 16)
                e.wait_ge(q["s_w1"], 32)
                for n in range(AHEAD):
                    e.wait_ge(s_ring[n], ring_need[n])
                e.wait_ge(q["s_yev"], NB)
                e.wait_ge(q["s_rev"], NB)
                y_stored(e, 0)
                e.sem_inc(token["DVE"], 1)
            emit(steps, None, None)

        block.sync(sync_engine)
        block.gpsimd(gpsimd_engine)
        block.tensor(tensor_engine)
        block.scalar(scalar_engine)
        block.vector(vector_engine)
    return nc


_INS = ["x", "src", "dst", "edge_type_4", "L0_gnn_weights", "L0_gnn_roots", "L0_gnn_biases"]


def kernel(**inputs):
    import concourse.bacc as _bacc
    from concourse.bass_utils import run_bass_kernel_spmd as _run

    nc = _bacc.Bacc("TRN2", target_bir_lowering=False, num_devices=1)
    arrays, args = {}, []
    given = {n: np.ascontiguousarray(inputs[n]) for n in _INS}
    given.update(constants(given["x"].shape[0], given["src"].shape[0]))
    for name, a in given.items():
        arrays[f"in_{name}"] = a
        args.append(nc.dram_tensor(f"in_{name}", a.shape, mybir.dt.from_np(a.dtype), kind="ExternalInput").ap())
    o = nc.dram_tensor("out_0", given["x"].shape, F32, kind="ExternalOutput").ap()
    rgcn_kernel(nc, *args, o)
    r = _run(nc, [arrays], core_ids=[0])
    return r.results[0]["out_0"]
```

```python
import math

import numpy as np
import concourse.bass as bass
import concourse.mybir as mybir
from contextlib import ExitStack

F32 = mybir.dt.float32
I32 = mybir.dt.int32
U8 = mybir.dt.uint8
BF16 = mybir.dt.bfloat16
F16 = mybir.dt.float16
ALU = mybir.AluOpType
ACT = mybir.ActivationFunctionType
AX = mybir.AxisListType

P = 128
D = 128
NR = 4
NL = 3
RW = 1024
FAR = 1000000
EPS = 1e-5
WINDOWS = 8
SPAN = 116
START_PE, START_POOL = 195.0, 215.0
CH = 5


class Plan:

    def __init__(self, N, E):
        self.N, self.E = N, E
        self.NP = NP = -(-E // RW)
        self.NG = NG = -(-E // 512)
        self.NT = -(-E // P)
        self.NB = NB = -(-N // P)
        node = lambda g: N * (g / NG) ** 2
        self.need = [max(0, int((node(g) - 96) // P)) for g in range(2 * NP)]
        self.win = []
        g = 0
        while len(self.win) < WINDOWS:
            h = g
            while h + 1 < NG // 2 and node(h + 1) - node(g) <= SPAN:
                h += 1
            if h == g:
                break
            m = (h - g) * 512 * P / N
            self.win.append((g, h, math.ceil((m + 4.8 * math.sqrt(m)) / P)))
            g = h
        self.G1 = g
        self.TH = 4 * g
        self.slot0, n = [], 0
        for _, _, c in self.win:
            self.slot0.append(n)
            n += c * NB
        self.NSL = n
        last = self.win[-1][0]
        self.KH = min(NB, max(int(node(last) + 40) // P + 2, int(node(g) + 40) // P + 1))
        self.most = np.full(2 * NP, 2.0 * FAR, np.float32)
        self.most[last] = P * (self.KH - 1)
        if g < NG:
            self.most[g] = min(self.most[g], P * self.KH - 1)
        self.chunks = [list(range(a, min(a + CH, NB))) for a in range(0, NB, CH)]
        self.phases, cur = [], []
        for w, (a, b, _) in enumerate(self.win):
            if cur and (b - self.win[cur[0]][0]) * 4 > 110:
                self.phases.append(cur)
                cur = []
            cur.append(w)
        self.phases.append(cur)
        self.SCW = max(4 * (self.win[p[-1]][1] - self.win[p[0]][0]) for p in self.phases)


def constants(N, E):
    pl = Plan(N, E)
    e = np.arange(P, dtype=np.float32)
    base, cap = [], []
    for w, (_, _, c) in enumerate(pl.win):
        for b in range(pl.NB):
            base.append((pl.slot0[w] + b * c) * P)
            cap.append(c * P)
    return {
        "c_ident": np.eye(P, dtype=np.float32),
        "c_iota": np.tile(e, (P, 1)),
        "c_tri": np.stack([(e[None, :] < e[:, None]), (e[:, None] < e[None, :])], 1).astype(np.float32),
        "c_col": np.stack([N + e, NR * N + e], 1).astype(np.float32),
        "c_valid": (np.arange(pl.NP * RW).reshape(pl.NP, RW) < E).astype(np.float32),
        "c_need": (P * np.array(pl.need, np.float32)).reshape(pl.NP, 2),
        "c_most": pl.most.reshape(pl.NP, 2),
        "c_iota16": np.tile(np.arange(NR * P, dtype=np.float16), (P, 1)),
        "c_bucket": np.tile(np.array([base, cap], np.float32)[None], (P, 1, 1)),
    }


def schedule(pl, R):
    gather, land = 1.04, 2.5
    sparse = list(range(pl.G1, pl.NG))
    NS, W, NCH = len(sparse), len(pl.win), len(pl.chunks)
    ntile = [min(4, pl.NT - 4 * g) for g in sparse]
    pieces = [(w, g) for w, (a, b, _) in enumerate(pl.win) for g in range(a, b)]
    layers, pools = [], []
    for li in range(NL):
        pe = pool = 0.0
        queue, left = [], []
        arrive, recorded, eaten = [], {}, []
        if li == 0:
            queue = [("R", 0, g) for w, g in pieces if w == 0]
            left = [p for p in pieces if p[0]]
            queue += [("S", n) for n in range(min(R, NS))]
            arrive = [0.0] * min(R, NS)
            recorded[0] = 0.0
            pe, pool = START_PE, START_POOL
        items = []
        dense, NX = [], -(-pl.NB // 4)
        if li:
            dense += [("X", b) for b in range(NX)]
        for w in range(W):
            for k in range(NCH):
                if w == 0 and li == 0:
                    got = sum(it[0] == "X" for it in dense)
                    dense += [("X", b) for b in range(got, NX)]
                dense.append(("C", w, k))
                if li == 0 and k == max(0, NCH - 3):
                    dense.append(("N", w))
                if li == 0 and k == max(0, NCH - 2):
                    if w == 0:
                        got = sum(it[0] == "X" for it in dense)
                        dense += [("X", b) for b in range(got, NX)]
                    dense.append(("M", w))
            dense += [("F", w), ("G", w)]
        started = 0
        done, late = pl.KH, list(range(pl.KH))
        late0 = set(late)
        loaded = 0

        def step_pool():
            nonlocal pool
            n = len(arrive)
            can = n < NS and (n < R or n - R < len(eaten))
            at = max(pool, eaten[n - R] if can and n >= R else 0.0)
            hungry = left and len(recorded) - (left[0][1] > pl.win[left[0][0]][0]) < started + 1
            if left and (not can or at > pool + 1.0 or hungry):
                w, g = left.pop(0)
                queue.append(("R", w, g))
                pool += 4 * gather
                if g == pl.win[w][1] - 1:
                    recorded[w] = pool + 2 * land
                return True
            if not can:
                return False
            queue.append(("S", n))
            pool = at + ntile[n] * gather
            arrive.append(pool + land)
            return True

        wait_g = None
        while True:
            while pool <= pe + 2 and step_pool():
                pass
            while loaded in recorded and li == 0 and recorded[loaded] <= pe:
                items.append(("R", loaded))
                loaded += 1
            n = len(eaten)
            full = pl.NB if n == NS else min(pl.need[sparse[n - 1]], pl.NB) if n > 1 else 0
            nx = dense[0] if dense else None
            if nx and nx[0] == "C" and li == 0 and loaded <= nx[1]:
                nx = None
            x_done = not any(it[0] == "X" for it in dense)
            if n < len(arrive) and arrive[n] <= pe and not (dense and dense[0][0] == "X"):
                pe += 0.22 * ntile[n] + 0.1
                eaten.append(pe + 0.3)
                items.append(("S", n))
            elif x_done and li < NL - 1 and done < full:
                items.append(("E", done))
                done += 1
                pe += 1.5
            elif li == NL - 1 and x_done and done < full and (full - done >= 4 or full == pl.NB):
                take = min(4, full - done)
                items.append(("L", tuple(range(done, done + take))))
                done += take
                pe += 0.9
            elif not dense and late and full >= pl.KH:
                if li < NL - 1:
                    items += [("E", k) for k in late]
                    pe += 1.2 * len(late)
                else:
                    items += [("L", tuple(late[a:a + 4])) for a in range(0, len(late), 4)]
                    pe += 0.25 * len(late)
                late = []
            elif nx:
                dense.pop(0)
                items.append(nx)
                if nx[0] == "X":
                    pe += 1.5
                elif nx[0] == "C":
                    started = max(started, nx[1] + 1)
                    c = pl.win[nx[1]][2]
                    pe += len(pl.chunks[nx[2]]) * (0.70 + (0.12 + 0.24 * c if li == 0 else 0))
                elif nx[0] in "FM":
                    pe += 0.5
                elif nx[0] == "N":
                    pass
                else:
                    pe += 1.0
            elif n < NS or dense:
                ahead = []
                if n < len(arrive):
                    ahead.append(arrive[n])
                if li == 0 and loaded in recorded:
                    ahead.append(recorded[loaded])
                if ahead and min(ahead) > pe:
                    pe = min(ahead)
                else:
                    assert step_pool()
            elif late or done < pl.NB:
                raise AssertionError
            else:
                break
        for w in range(W - 1):
            at, to = items.index(("G", w)), items.index(("C", w + 1, 0))
            if not any(it[0] in "EL" and it[1] in late0 for it in items[at:to]):
                items.insert(to, items.pop(at))
        layers.append(items)
        pools.append(queue)
    return layers, pools


def rgcn_kernel(nc, x, src, dst, typ, weights, roots, biases, c_ident, c_iota, c_tri, c_col, c_valid, c_need,
                c_most, c_iota16, c_bucket, out):
    N, E = x.shape[0], src.shape[0]
    pl = Plan(N, E)
    NP, NG, NT, NB, NSL, TH = pl.NP, pl.NG, pl.NT, pl.NB, pl.NSL, pl.TH
    NT4 = NP * 8
    NW = NB * P + P
    NK = NR * N
    R = 12
    NS = 3
    YS = 4
    NO = 6
    AS = 3
    NZ = 4
    FULL = E // RW
    REST = E - FULL * RW
    W = len(pl.win)
    NCH = len(pl.chunks)
    NX = -(-NB // 4)
    bw = [min(P, N - k * P) for k in range(NB)]
    sparse = list(range(pl.G1, NG))
    NSG = len(sparse)
    tiles = {g: [t for t in range(4 * g, 4 * g + 4) if t < NT] for g in range(NG)}
    rows_of = [min(P, E - t * P) for t in range(NT)]
    layers, pools = schedule(pl, R)

    acc_total = 0
    acc_at, acc_of, t_uses = {}, {}, []
    ta = tv = 0
    for k in range(NB):
        ta += 1
        t_uses.append(("s_tA", ta))
    t_of, lasts = {}, []
    for li, items in enumerate(layers):
        for n, it in enumerate(items):
            acc_at[li, n] = acc_total
            if it[0] in "SG":
                acc_total += 1
                acc_of[li, it] = acc_total
            elif it[0] == "C" and li == 0:
                for i in pl.chunks[it[2]]:
                    t_of[li, it, i] = len(t_uses)
                    ta += 1
                    t_uses.append(("s_tA", ta))
            elif it[0] == "X" and li > 0:
                t_of[li, it] = len(t_uses)
                t_uses.append(("s_xv", li * NX + it[1] + 1))
            elif it[0] == "L":
                t_of[li, it] = len(t_uses)
                tv += 1
                t_uses.append(("s_tV", tv))
                lasts.append(it[1])
    def added(li, pos):
        k = layers[li][pos][1]
        if k < pl.KH:
            return acc_at[li, pos]
        last = max([n for n, g in enumerate(sparse) if pl.need[g] <= k])
        return acc_of[li, ("S", last)]

    y_no = {(0, k): k for k in range(NB)}
    for li, items in enumerate(layers):
        for it in items:
            if it[0] == "E":
                y_no[li + 1, it[1]] = len(y_no)
    g_uses, g_of = [], {}
    for li, items in enumerate(layers):
        for it in items:
            if it[0] in "SG":
                g_of[li, it] = len(g_uses)
                g_uses.append(("s_acc", acc_of[li, it]))
            elif it[0] == "E":
                g_of[li, it] = len(g_uses)
                g_uses.append(("s_rev", y_no[li + 1, it[1]] + 1))
    chunk_no = {}
    for li, items in enumerate(layers):
        for it in items:
            if it[0] == "C":
                chunk_no[li, it] = len(chunk_no)
    x_no = {(li, ("X", b)): li * NX + b for li in range(NL) for b in range(NX)}
    f_no = {(li, ("F", w)): li * W + w for li in range(NL) for w in range(W)}
    pairs, first_of, of_block = [], {}, {}
    for it in layers[0]:
        if it[0] == "C":
            _, w, k = it
            a, b, c = pl.win[w]
            first_of[it] = len(pairs)
            blocks = pl.chunks[max(0, NCH - 3)][-1] + 1
            for i in pl.chunks[k]:
                of_block[w, i] = len(pairs)
                pairs += [("A", w, i, j) for j in range(c)]
                n = 4 * (b - a)
                if i < blocks:
                    pairs += [("N", w, t, None) for t in range(4 * a + n * i // blocks, 4 * a + n * (i + 1) // blocks)]
            first_of[it, "end"] = len(pairs)

    ctx = ExitStack()
    with ctx:
        sb = lambda name, shape, dt=F32: ctx.enter_context(nc.sbuf_tensor(name, shape, dt))
        ps = lambda name, shape: ctx.enter_context(nc.psum_tensor(name, shape, F32))
        sem = lambda name: ctx.enter_context(nc.semaphore(name))
        ctx.enter_context(nc.allow_non_contiguous_dma("the biases, one element a partition"))

        Y = [nc.dram_tensor(f"ytab{i}", [NK, D], F32).ap() for i in range(2)]
        acc_dram = nc.dram_tensor("acc_dram", [(NB + 1) * P, D], F32).ap()
        NC = -(-(NK + P) // P)
        cnt_dram = nc.dram_tensor("cnt_dram", [NC * P, 1], F32).ap()
        cf_dram = nc.dram_tensor("cf_dram", [NP, 2 * NR], F32).ap()
        over = max(b - a for a, b, _ in pl.win) * 512
        rec_dram = nc.dram_tensor("rec_dram", [NSL * P + over, 2], F32).ap()
        a_dram = [nc.dram_tensor(f"a_dram{w}", [P, NB * NR * P], F16).ap() for w in range(W)]

        ident, iota, tri = sb("ident", [P, P]), sb("iota", [P, P]), sb("tri", [P, 2, P])
        lower, upper = tri[:, 0, :], tri[:, 1, :]
        dumpc = sb("dumpc", [P, 2])
        iota16 = sb("iota16", [P, NR * P], F16)
        onesf = sb("onesf", [P, P])
        need_t, most_t = sb("need_t", [NP, 2]), sb("most_t", [NP, 2])
        ends = sb("ends", [NP, 2, 2, NR])
        carry = sb("carry", [NR, 2, NP + 2])
        cin = sb("cin", [NP, 2, NR])
        chk = sb("chk", [NP, 8])
        viol = sb("viol", [P, 4])
        basew = sb("basew", [P, W + 1])
        starts = [g for g, _, _ in pl.win] + [pl.G1]
        NF = starts[-1] // 2 + 1
        cfirst = sb("cfirst", [NP, 2, NR])
        cfb = sb("cfb", [P, NF, 2, NR])
        delta = sb("delta", [P, W])
        flag_i = sb("flag_i", [1, 1], I32)
        brow = sb("brow", [1, 2, NP], I32)
        idxc = sb("idxc", [P, NT4], I32)
        relc, wc, dstc = sb("relc", [P, NT4]), sb("wc", [P, NT4]), sb("dstc", [P, NT4])
        posc = sb("posc", [P, TH], I32)
        recv = sb("recv", [P, TH, 2])
        B = [sb("node0", [P, NW]), sb("node1", [P, NW])]
        wt = sb("wt", [P, NL, NR, D])
        rt = sb("rt", [P, NL, D])
        bt = sb("bt", [P, NL])
        ring = sb("ring", [P, max(R * 512, NB * P)])
        S = sb("S", [P, NS, 4, P])
        yst = sb("yst", [P, YS, NR * D])
        tmask = sb("tmask", [P, TH, NR], BF16)
        cn = sb("cn", [NR, P])
        recs = sb("recs", [P, NSL, 2])
        V = sb("V", [P, max(4 * W * NB, NR * P + NO * (1 + NR) * P // 2, 3 * NR * P)])
        bucket = V[:, 0:2 * W * NB].rearrange("p (a b) -> p a b", a=2)
        tot = V[:, 2 * W * NB:3 * W * NB].rearrange("p (w b) -> p w b", b=NB)
        offs = V[:, 3 * W * NB:4 * W * NB].rearrange("p (w b) -> p w b", b=NB)
        assert 3 * TH + 4 * (NP + 2) <= NS * 4 * P
        sv = S[:].rearrange("p s i c -> p (s i c)")
        blk, tmpi, relw = (sv[:, i * TH:(i + 1) * TH] for i in range(3))
        blk, tmpi = blk.bitcast(I32), tmpi.bitcast(I32)
        rowt = sv[0:NR, 3 * TH:3 * TH + 4 * (NP + 2)].rearrange("r (a b c) -> r a b c", a=2, b=2)
        ms, left = V[:, 0:NR * P], V[:, NR * P:3 * NR * P]
        oh = V[:, NR * P:NR * P + NO * (1 + NR) * P // 2].bitcast(BF16).rearrange("p (v c) -> p v c", v=NO)
        ohs, ohk = oh[:, :, 0:P], oh[:, :, P:(1 + NR) * P]
        st = sb("st", [P, 4, 6])
        mv = sb("mv", [P, 4, 2])
        sd = sb("sd", [P, 4])
        rs = sb("rs", [P, 4])
        epst = sb("epst", [P, 1])
        xn = ring[:, 0:NB * P].rearrange("p (k f) -> p k f", f=D)
        zx = yst[:].rearrange("p s (j f) -> p s j f", f=D)

        scn = NB * pl.SCW
        early = 10 * RW + scn + 1 + -(-scn // 4)
        xw, aw, cw = 3 * NB * P // 2, AS * CH * NR * P // 2, W * NR * P
        U = sb("U", [P, max(early, xw + aw + cw)])
        row = lambda i, dt=F32: U[0:NP, i * RW:(i + 1) * RW].bitcast(dt)
        a_dst, a_typ, a_prev, a_next, a_src = (row(i, I32) for i in range(5))
        valid, a_idx, a_dstf, a_rel, a_w = (row(i) for i in range(5, 10))
        same_p, same_n, mask, fwd, bwd = row(2), row(3), row(4), row(6), row(7)
        sc = U[:, 10 * RW:10 * RW + scn + 1]
        m8 = U[:, 10 * RW + scn + 1:10 * RW + scn + 1 + -(-scn // 4)].bitcast(U8)
        xs = U[:, 0:xw].bitcast(BF16).rearrange("p (s k f) -> p s k f", s=3, f=D)
        aring = U[:, xw:xw + aw].bitcast(F16).rearrange("p (s i c) -> p s i c", s=AS, c=NR * P)
        cinv = U[:, xw + aw:xw + aw + cw].rearrange("p (w c) -> p w c", c=NR * P)

        psGR, psRB = ps("psGR", [P, 512]), ps("psRB", [P, 512])
        psG, psR = psGR[:, 0:P], psRB[:, 0:P]
        part = [psG, psR]
        psY = [ps("psY0", [P, 512]), ps("psY1", [P, 512])]
        psT = [ps("psT0", [P, 512]), ps("psT1", [P, 512])]
        psD, psB = ps("psD", [P, 512]), ps("psB", [P, 512])
        psC = [psD, psB]

        names = ("s_e0 s_e1 s_e2 s_c s_x0 s_x1 s_w0 s_w1 s_fill s_v s_tp s_tev s_fl s_br s_small s_sm s_st s_xt "
                 "s_ym s_rm s_yev s_rev s_tA s_tV s_S s_pe s_acc s_fin s_sq s_sd s_no s_v2 s_v3 s_pos s_pf "
                 "s_rl s_bd s_oh s_dn s_fd s_fp s_xa s_xv s_xl s_dead tSP tPE tACT tDVE tPOOL gd gp s_cf s_rf s_xc s_xw s_n1 s_n2 s_n3").split()
        q = {n: sem(n) for n in names}
        s_ring = [sem(f"s_ring{i}") for i in range(R)]
        s_yd = [sem(f"s_yd{i}") for i in range(YS)]
        s_as = [sem(f"s_as{i}") for i in range(AS)]
        s_z = [sem(f"s_z{i}") for i in range(NZ)]
        s_sc = [sem(f"s_sc{w}") for w in range(W)]
        s_xs = [sem(f"s_xs{i}") for i in range(W)]
        block = ctx.enter_context(nc.Block())

        base_ap = brow[:].rearrange("a h p -> a (h p)")
        base_col = lambda g: (g % 2) * NP + g // 2
        dview = dst.rearrange("(a e) -> a e", a=1)
        nxt0 = min(7, NB - 2)

        def node_src(li):
            return B[li % 2], B[(li + 1) % 2]

        def g_bank(e, u):
            if u >= 2:
                s, count = g_uses[u - 2]
                e.wait_ge(q[s], count)
            return part[u % 2]

        def t_free(e, u):
            if u >= 2:
                s, count = t_uses[u - 2]
                e.wait_ge(q[s], count)

        n_rows = 1 + (REST > 0)
        n1 = FULL if REST else FULL - 1
        last_n = E - 1 - n1 * RW
        N_E0 = 16 * (2 * n_rows + 2)
        N_E1 = 16 * (n_rows + 1 + (FULL > 1) + (REST > 0) + 6)
        N_E2 = 16 * (1 + (last_n > 0))

        def store_y(e, li, k):
            n = y_no[li, k]
            e.wait_ge(q["s_yev"], n + 1)
            e.dma_start(Y[li % 2][NR * P * k:NR * (P * k + bw[k]), :].rearrange("(n r) f -> n (r f)", r=NR),
                        yst[0:bw[k], n % YS, :]).then_inc(s_yd[n % YS], 16)

        def y_stored(e, li):
            for s in range(YS):
                e.wait_ge(s_yd[s], 16 * len(range(s, (li + 1) * NB, YS)))

        def a_view(w, k):
            ks = pl.chunks[k]
            return a_dram[w][:, ks[0] * NR * P:(ks[-1] + 1) * NR * P].rearrange("p (i c) -> p i c", c=NR * P)

        def load_rows(e, t, ap, s):
            e.dma_start(t[0:FULL, :], ap[0:FULL * RW].rearrange("(p j) -> p j", j=RW)).then_inc(s, 16)
            if REST:
                e.dma_start(t[FULL:FULL + 1, 0:REST], ap[FULL * RW:E].rearrange("(a j) -> a j", a=1)).then_inc(s, 16)

        def sync_engine(e):
            e.dma_start(ident[:], c_ident).then_inc(q["s_c"], 16)
            e.dma_start(xn[:, 0:nxt0, :], x[0:nxt0 * P, :].rearrange("(k p) f -> p k f", p=P)).then_inc(q["s_x0"], 16)
            e.dma_start(wt[:, 0], weights[0].rearrange("r i o -> i r o")).then_inc(q["s_w0"], 16)
            e.dma_start(rt[:, 0], roots[0]).then_inc(q["s_w0"], 16)
            e.dma_start(bt[:], biases.rearrange("l o -> o l")).then_inc(q["s_w0"], 16)
            e.wait_ge(q["s_fill"], 1)
            load_rows(e, a_src, src, q["s_e0"])
            load_rows(e, a_typ, typ, q["s_e0"])
            e.dma_start(iota[:], c_iota).then_inc(q["s_e0"], 16)
            e.dma_start(bucket, c_bucket).then_inc(q["s_e0"], 16)
            load_rows(e, a_dst, dst, q["s_e1"])
            nf = N // P
            e.dma_start(xn[:, nxt0:nf, :], x[nxt0 * P:nf * P, :].rearrange("(k p) f -> p k f", p=P)).then_inc(q["s_x1"], 16)
            if nf < NB:
                e.dma_start(xn[0:bw[-1], NB - 1, :], x[nf * P:N, :]).then_inc(q["s_x1"], 16)
            e.dma_start(a_prev[0:1, 1:RW], dview[:, 0:RW - 1]).then_inc(q["s_e1"], 16)
            if FULL > 1:
                e.dma_start(a_prev[1:FULL, :], dst[RW - 1:FULL * RW - 1].rearrange("(p j) -> p j", j=RW)).then_inc(q["s_e1"], 16)
            if REST:
                e.dma_start(a_prev[FULL:FULL + 1, 0:REST], dview[:, FULL * RW - 1:E - 1]).then_inc(q["s_e1"], 16)
            for t, c in ((need_t, c_need), (most_t, c_most), (valid, c_valid), (tri, c_tri),
                         (dumpc, c_col), (iota16, c_iota16)):
                e.dma_start(t if t is valid else t[:], c).then_inc(q["s_e1"], 16)
            e.dma_start(a_next[0:n1, :], dst[1:1 + n1 * RW].rearrange("(p j) -> p j", j=RW)).then_inc(q["s_e2"], 16)
            if last_n:
                e.dma_start(a_next[n1:n1 + 1, 0:last_n], dview[:, n1 * RW + 1:E]).then_inc(q["s_e2"], 16)
            e.dma_start(wt[:, 1:3].rearrange("i l r o -> i (l r) o"), weights[1:3].rearrange("l r i o -> i (l r) o")).then_inc(q["s_w1"], 16)
            e.dma_start(rt[:, 1:3], roots[1:3].rearrange("l i o -> i l o")).then_inc(q["s_w1"], 16)
            e.wait_ge(q["s_rf"], 1)
            e.dma_start(rec_dram[0:NSL * P, :].rearrange("(p c) a -> p (c a)", p=P), recs[:].rearrange("p c a -> p (c a)")).then_inc(q["s_pf"], 16)
            for k in range(NB):
                store_y(e, 0, k)
            branch(e, "SP", sp_fast)

        z_uses = {}

        def z_plan():
            total = [0] * NZ
            for b, ks in enumerate(lasts):
                parts = 1 if (bw[ks[-1]] == P or len(ks) == 1) else 2
                total[b % NZ] += 16 * parts
                load = total[b % NZ]
                total[b % NZ] += 16 * parts
                z_uses[b] = (load, total[b % NZ])
            return total

        z_total = z_plan()

        def z_parts(ks):
            full = [k for k in ks if bw[k] == P]
            parts = [(0, len(full), P)] if full else []
            if len(full) < len(ks):
                parts.append((len(full), len(ks), bw[ks[-1]]))
            return parts

        def node_rows(t, k0, m, rr):
            if rr == P:
                return t[P * k0:P * (k0 + m), :].rearrange("(k p) f -> p k f", p=P)
            return t[P * k0:P * k0 + rr, :].rearrange("(k p) f -> p k f", k=1)

        def sp_fast(e):
            def load_chunk(li, w, k):
                cc = chunk_no[li, ("C", w, k)]
                e.wait_ge(q["s_dn"], cc - AS + 1)
                e.wait_ge(s_as[cc % AS], 16 * (cc // AS))
                e.dma_start(aring[:, cc % AS, 0:len(pl.chunks[k]), :], a_view(w, k)).then_inc(s_as[cc % AS], 16)

            order = [(w, k) for w in range(W) for k in range(NCH)]
            def x_load(b):
                ks = list(range(4 * b, min(4 * b + 4, NB)))
                for a, c, rr in z_parts(ks):
                    e.dma_start(cinv[0:rr, b % W, a * P:c * P].rearrange("p (k f) -> p k f", f=D),
                                node_rows(x, ks[a], c - a, rr)).then_inc(s_xs[b % W], 16)

            e.wait_ge(q["s_tev"], 4)
            for b in range(min(W, NX)):
                x_load(b)
            for li, items in enumerate(layers):
                if li:
                    if li == 1:
                        for s in range(AS):
                            e.wait_ge(s_as[s], 16 * len(range(s, W * NCH, AS)))
                    for w, k in order[0:2]:
                        load_chunk(li, w, k)
                zb = 0

                def z_load(b):
                    ks = lasts[b]
                    if b >= NZ:
                        e.wait_ge(s_z[b % NZ], z_uses[b - NZ][1])
                    for a, c, rr in z_parts(ks):
                        e.dma_start(zx[0:rr, b % NZ, a:c, :], node_rows(x, ks[a], c - a, rr)).then_inc(s_z[b % NZ], 16)

                if li == NL - 1:
                    y_stored(e, NL - 1)
                    for b in range(min(NZ - 1, len(lasts))):
                        z_load(b)
                for it in items:
                    if it[0] == "R":
                        w = it[1]
                        c = pl.win[w][2]
                        e.wait_ge(s_sc[w], 16 * 4 * (pl.win[w][1] - pl.win[w][0]))
                        lo = pl.slot0[w]
                        e.dma_start(recs[:, lo:lo + NB * c, :].rearrange("p (i c) a -> p i (c a)", c=c),
                                    rec_dram[lo * P:(lo + NB * c) * P, :].rearrange("(i p c) a -> p i (c a)", p=P, c=c)
                                    ).then_inc(q["s_rl"], 16)
                        e.wait_ge(q["s_rl"], 16 * (w + 1))
                    elif it[0] == "X" and li == 0:
                        if it[1] + W < NX:
                            e.wait_ge(q["s_xw"], it[1] + 1)
                            x_load(it[1] + W)
                    elif it[0] == "C":
                        _, w, k = it
                        cc = chunk_no[li, it]
                        if li == 0:
                            i = pl.chunks[k][-1]
                            e.wait_ge(q["s_tA"], t_uses[t_of[li, it, i]][1])
                            e.dma_start(a_view(w, k), aring[:, cc % AS, 0:len(pl.chunks[k]), :]).then_inc(s_as[cc % AS], 16)
                        else:
                            at = w * NCH + k + 2
                            if at < len(order):
                                load_chunk(li, *order[at])
                    elif it[0] == "E":
                        store_y(e, li + 1, it[1])
                    elif it[0] == "L":
                        b = zb
                        zb += 1
                        e.wait_ge(q["s_no"], b + 1)
                        for a, c, rr in z_parts(it[1]):
                            e.dma_start(node_rows(out, it[1][a], c - a, rr), zx[0:rr, b % NZ, a:c, :]).then_inc(s_z[b % NZ], 16)
                        if b + NZ - 1 < len(lasts):
                            z_load(b + NZ - 1)
            for s in range(NZ):
                e.wait_ge(s_z[s], z_total[s])

        def branch(e, name, fast):
            e.wait_ge(q["s_fl"], 1)
            v = e.value_load(flag_i[0:1, 0:1], min_val=0, max_val=4 * P)
            with e.If(v < 1):
                fast(e)
            with e.Else():
                general(e, name)

        ring_total = [0] * R
        ring_need = {}
        for li in range(NL):
            for s in range(NSG):
                n = li * NSG + s
                ring_total[n % R] += 16 * len(tiles[sparse[s]])
                ring_need[n] = ring_total[n % R]
        AHEAD = min(R, NSG)
        FIRST = pl.win[0][1] + AHEAD

        def gather(e, li, s):
            n = li * NSG + s
            if n >= R:
                e.wait_ge(q["s_pe"], n - R + 1)
            for i, t in enumerate(tiles[sparse[s]]):
                m = rows_of[t]
                at = (n % R) * 512 + i * P
                e.indirect_dma_start(ring[0:m, at:at + P], None, Y[li % 2],
                                     bass.IndirectOffsetOnAxis(ap=idxc[0:m, t:t + 1], axis=0)
                                     ).then_inc(s_ring[n % R], 16)

        def gpsimd_engine(e):
            tail = FULL // 32 * 32
            e.memset(a_src[tail:NP, :], 0)
            e.memset(a_typ[tail:NP, :], 0)
            e.memset(a_dst[tail:NP, :], FAR)
            e.memset(a_next[tail:NP, :], FAR)
            last = e.memset(a_prev[tail:NP, :], -1)
            if tail:
                last = e.memset(a_prev[0:1, 0:1], -1)
            last.then_inc(q["s_fill"], 1)
            e.wait_ge(q["s_pf"], 16)
            for what in pools[0][:FIRST]:
                if what == ("S", 0):
                    e.wait_ge(q["s_tev"], 1)
                    y_stored(e, 0)
                pool_part(e, 0, what)
            branch(e, "POOL", pool_fast)

        def pool_part(e, li, what):
            if what[0] == "S":
                gather(e, li, what[1])
                return
            _, w, g = what
            e.wait_ge(q["s_pos"], [i for i, p in enumerate(pl.phases) if w in p][0] + 1)
            for t in range(4 * g, 4 * g + 4):
                e.indirect_dma_start(rec_dram, bass.IndirectOffsetOnAxis(ap=posc[:, t:t + 1], axis=0),
                                     recv[:, t, :], None).then_inc(s_sc[w], 16)

        def pool_fast(e):
            for li in range(NL):
                if li:
                    y_stored(e, li)
                for what in pools[li][0 if li else FIRST:]:
                    pool_part(e, li, what)

        def pe_block(e, li, k):
            n = y_no[li, k]
            src_b, _ = node_src(li)
            h = src_b[:, P * k:P * k + bw[k]]
            if li == 0:
                e.wait_ge(q["s_tA"], n + 1)
            else:
                e.wait_ge(q["s_xt"], n - NB + 1)
            if n >= 2:
                e.wait_ge(q["s_yev"], n - 1)
            e.matmul(psY[n % 2][0:bw[k], :], h, wt[:, li].rearrange("i r o -> i (r o)"),
                     start=True, stop=True).then_inc(q["s_ym"], 1)
            if li == 0:
                e.wait_ge(q["s_rev"], n)
                root = psR
            else:
                root = g_bank(e, g_of[li - 1, ("E", k)])
            e.matmul(root[:, 0:bw[k]], rt[:, li, :], h, start=True, stop=True).then_inc(q["s_rm"], 1)

        def pe_cols(e, a):
            for qd in range(8):
                last = e.transpose(psC[qd // 4][:, (qd % 4) * NP:(qd % 4 + 1) * NP], a[:, P * qd:P * (qd + 1)],
                                   ident[0:NP, 0:NP])
            last.then_inc(q["s_tp"], 1)

        small = [0]

        def pe_small(e, *products):
            e.wait_ge(q["s_sm"], small[0])
            for o, a, b in products:
                last = e.matmul(o, a, b, start=True, stop=True)
            small[0] += 1
            last.then_inc(q["s_small"], 1)

        def pe_rank(e, i):
            w0, w1 = pl.phases[i][0], pl.phases[i][-1] + 1
            t = tot[:, w0:w1, :].rearrange("p w b -> p (w b)")
            e.wait_ge(q["s_v"], 5 + i)
            n = (w1 - w0) * NB
            bases = [(psGR[:, 400 + w:401 + w], onesf[0:1, :], dstc[0:1, 4 * g:4 * g + 1])
                     for w, g in enumerate(starts)] if i == 0 else []
            pe_small(e, *bases, (psGR[:, 0:n], upper, t), (psGR[:, 200:200 + n], onesf[:], t))

        def tensor_engine(e):
            def xt(k):
                if k == 0:
                    e.wait_ge(q["s_c"], 16)
                    e.wait_ge(q["s_x0"], 16)
                if k == nxt0:
                    e.wait_ge(q["s_x1"], 16 * (1 + (N % P > 0)))
                t_free(e, k)
                e.transpose(psT[k % 2][:, 0:bw[k]], xn[0:bw[k], k, :], ident[0:bw[k], 0:bw[k]]).then_inc(q["s_st"], 1)

            xt(0)
            xt(1)
            e.wait_ge(q["s_w0"], 48)
            NPH = len(pl.phases)
            for k in range(NB):
                pe_block(e, 0, k)
                if k + 2 < NB:
                    xt(k + 2)
                if k == min(1, NB - 1):
                    e.wait_ge(q["s_v"], 1)
                    pe_cols(e, a_idx)
                if k == min(5, NB - 1):
                    e.wait_ge(q["s_v"], 3)
                    for n, a in enumerate((a_dstf, a_rel)):
                        e.wait_ge(q["s_tev"], 1 + n)
                        pe_cols(e, a)
                for i in range(NPH):
                    if k == min((6, 31, 48)[min(i, 2)], NB - 1):
                        pe_rank(e, i)
            e.wait_ge(q["s_v"], 5 + NPH)
            pe_small(e, (psGR[0:1, 410:411], viol[:, 3:4], onesf[:, 0:1]),
                     *[(psGR[0:1, h * NP:(h + 1) * NP], chk[:, 5 + h:6 + h], ident[0:NP, 0:NP]) for h in range(2)])
            e.wait_ge(q["s_tev"], 3)
            e.wait_ge(q["s_v"], 6 + NPH)
            for d in range(2):
                for w in range(2):
                    last = e.transpose(psC[d][0:NR, w * NP:(w + 1) * NP], ends[:, d, w, :], ident[0:NP, 0:NP])
            last.then_inc(q["s_tp"], 1)
            e.wait_ge(q["s_v"], 7 + NPH)
            for d in range(2):
                c = carry[:, d, 0:NP] if d == 0 else carry[:, d, 1:NP + 1]
                last = e.transpose(psC[d][0:NP, 256:256 + NR], c, ident[0:NR, 0:NR])
            last.then_inc(q["s_tp"], 1)
            e.wait_ge(q["s_v"], 8 + NPH)
            pe_cols(e, a_w)
            branch(e, "PE", pe_fast)

        def pe_fast(e):
            e.wait_ge(q["s_tev"], 4)
            e.wait_ge(q["s_sm"], 1 + len(pl.phases))
            e.wait_ge(q["s_w1"], 32)
            e.wait_ge(q["s_rev"], NB)
            for li, items in enumerate(layers):
                src_b, acc_b = node_src(li)
                for pos, it in enumerate(items):
                    if it[0] == "S":
                        n = li * NSG + it[1]
                        g = sparse[it[1]]
                        e.wait_ge(q["s_S"], n + 1)
                        o = g_bank(e, g_of[li, it])
                        e.wait_ge(s_ring[n % R], ring_need[n])
                        for i, t in enumerate(tiles[g]):
                            m = rows_of[t]
                            at = (n % R) * 512 + i * P
                            last = e.matmul(o, ring[0:m, at:at + P], S[0:m, n % NS, i, :],
                                            start=(i == 0), stop=(i == len(tiles[g]) - 1))
                        last.then_inc(q["s_pe"], 1)
                    elif it[0] == "E":
                        pe_block(e, li + 1, it[1])
                    elif it[0] == "X" and li:
                        u = t_of[li, it]
                        t_free(e, u)
                        ks = range(4 * it[1], min(4 * it[1] + 4, NB))
                        e.wait_ge(q["s_xt"], li * NB)
                        for j, k in enumerate(ks):
                            last = e.transpose(psT[u % 2][0:bw[k], j * D:(j + 1) * D],
                                               src_b[:, P * k:P * k + bw[k]], ident[:])
                        last.then_inc(q["s_st"], 1)
                    elif it[0] == "C":
                        pe_chunk(e, li, it)
                    elif it[0] == "M":
                        e.wait_ge(q["s_n1"], it[1] + 1)
                        for r in range(NR):
                            last = e.matmul(psB[:, r * P:(r + 1) * P], ident[0:NR, r:r + 1].to_broadcast([NR, P]), cn[:],
                                            start=True, stop=True)
                        last.then_inc(q["s_n2"], 1)
                    elif it[0] == "G":
                        f = f_no[li, ("F", it[1])]
                        e.wait_ge(q["s_fd"], f + 1)
                        o = g_bank(e, g_of[li, it])
                        for r in range(NR):
                            last = e.matmul(o, wt[:, li, r, :], ms[:, r * P:(r + 1) * P], start=(r == 0), stop=(r == NR - 1))
                        last.then_inc(q["s_fp"], 1)
                    elif it[0] == "L":
                        e.wait_ge(q["s_acc"], acc_at[li, pos])
                        u = t_of[li, it]
                        t_free(e, u)
                        for j, k in enumerate(it[1]):
                            last = e.transpose(psT[u % 2][0:bw[k], j * D:(j + 1) * D],
                                               acc_b[:, P * k:P * k + bw[k]], ident[:])
                        last.then_inc(q["s_fin"], 1)

        def pe_chunk(e, li, it):
            _, w, kc = it
            cc = chunk_no[li, it]
            slot = cc % AS
            ks = pl.chunks[kc]
            c = pl.win[w][2]
            f = f_no[li, ("F", w)]
            if kc == 0:
                e.wait_ge(q["s_fd"], f if f < W else max(W, f - 1))
                if li:
                    e.wait_ge(q["s_xw"], NX * (li + 1))
            if f == 0:
                e.wait_ge(q["s_xw"], ks[-1] // 4 + 1)

            bank = psD if li == 0 else psC[f % 2]

            def dense(i):
                m = bw[i]
                a = aring[0:m, slot, i - ks[0], :]
                if li == 0:
                    e.wait_ge(q["s_tA"], t_uses[t_of[li, it, i]][1])
                for s in range(3):
                    last = e.matmul(bank[:], xs[0:m, s, i, :], a, start=(i == 0 and s == 0), stop=(i == NB - 1 and s == 2))
                if i == ks[-1]:
                    last.then_inc(q["s_dn"], 1)

            if li:
                e.wait_ge(s_as[slot], 16 * (cc // AS + 1))
            for i in ks:
                if li == 0:
                    u = t_of[li, it, i]
                    t_free(e, u)
                    for j in range(c):
                        v = of_block[w, i] + j
                        e.wait_ge(q["s_oh"], v + 1)
                        e.matmul(psT[u % 2][:], ohs[:, v % NO, :], ohk[:, v % NO, :], start=(j == 0),
                                 stop=(j == c - 1)).then_inc(q["s_bd"], 1)
                    v = of_block[w, i] + c
                    if i == 0:
                        e.wait_ge(q["s_n3"], w)
                    while v < len(pairs) and pairs[v][0:2] == ("N", w):
                        t = pairs[v][2]
                        e.wait_ge(q["s_oh"], v + 1)
                        e.matmul(psB[0:NR, 0:P], tmask[:, t, :], ohs[:, v % NO, :], start=(t == 4 * pl.win[w][0]),
                                 stop=(t == 4 * pl.win[w][1] - 1)).then_inc(q["s_bd"], 1)
                        v += 1
                    if i > ks[0]:
                        dense(i - 1)
                else:
                    dense(i)
            if li == 0:
                dense(ks[-1])

        def act_out(e, li, k):
            n = y_no[li, k]
            _, dst_b = node_src(li)
            e.wait_ge(q["s_ym"], n + 1)
            if n >= YS:
                e.wait_ge(s_yd[n % YS], 16 * (n // YS))
            e.activation(yst[0:bw[k], n % YS, :], psY[n % 2][0:bw[k], :], ACT.Copy).then_inc(q["s_yev"], 1)
            e.wait_ge(q["s_rm"], n + 1)
            root = part[g_of[li - 1, ("E", k)] % 2] if li else psR
            e.activation(dst_b[:, P * k:P * k + bw[k]], root[:, 0:bw[k]], ACT.Identity,
                         bias=bt[:, li:li + 1]).then_inc(q["s_rev"], 1)

        def scalar_engine(e):
            def cp(k):
                e.wait_ge(q["s_st"], k + 1)
                e.activation(B[0][:, P * k:P * k + bw[k]], psT[k % 2][:, 0:bw[k]], ACT.Copy).then_inc(q["s_tA"], 1)
            for k in range(NB):
                if k == 0:
                    cp(0)
                if k + 1 < NB:
                    cp(k + 1)
                act_out(e, 0, k)
            branch(e, "ACT", act_fast)

        def act_fast(e):
            first_e = [it for it in layers[0] if it[0] == "E"][0]
            e.wait_ge(q["s_v"], 8 + len(pl.phases))
            e.dma_start(cf_dram, cfirst[:].rearrange("p h r -> p (h r)")).then_inc(q["s_cf"], 16)
            e.wait_ge(q["s_cf"], 16)
            e.dma_start(cfb[:].rearrange("p g h r -> p (g h r)"),
                        cf_dram[0:NF, :].rearrange("(a g) c -> a (g c)", a=1).to_broadcast([P, NF * 2 * NR])
                        ).then_inc(q["s_cf"], 16)
            lb = 0
            for li, items in enumerate(layers):
                started = set()
                if li:
                    e.wait_ge(q["s_xw"], NX)
                for pos, it in enumerate(items):
                    if li == 0 and it == first_e:
                        e.wait_ge(q["s_xw"], NX)
                    if it[0] == "E":
                        if items[pos - 1][0] == "E":
                            continue
                        run = []
                        while pos + len(run) < len(items) and items[pos + len(run)][0] == "E":
                            run.append(items[pos + len(run)][1])
                        for j, k in enumerate(run):
                            e.wait_ge(q["s_acc"], added(li, pos + j))
                            b = B[(li + 1) % 2][:, P * k:P * k + bw[k]]
                            e.activation(b, b, ACT.Relu).then_inc(q["s_xt"], 1)
                            if j:
                                act_out(e, li + 1, run[j - 1])
                        act_out(e, li + 1, run[-1])
                    elif it[0] == "X":
                        def first(it):
                            if it not in started:
                                started.add(it)
                                for a, c, rr, o, s_in, t_in in x_parts(e, li, it, "ACT"):
                                    last = e.activation(o(0), s_in, ACT.Copy)
                                last.then_inc(q["s_xa"], 1)

                        first(it)
                        if items[pos + 1][0] == "X":
                            first(items[pos + 1])
                        n = x_no[li, it]
                        e.wait_ge(q["s_xv"], n + 1)
                        for a, c, rr, o, s_in, t_in in x_parts(e, li, it, None):
                            last = e.activation(o(1), t_in, ACT.Copy)
                        last.then_inc(q["s_xc"], 1)
                    elif it[0] == "C" and li == 0:
                        _, w, kc = it
                        cc = chunk_no[li, it]
                        slot = cc % AS
                        c = pl.win[w][2]
                        if cc == 0:
                            e.wait_ge(q["s_tev"], 4)
                        if cc >= AS:
                            e.wait_ge(s_as[slot], 16 * (cc // AS))
                            e.wait_ge(q["s_dn"], cc - AS + 1)
                        for i in pl.chunks[kc]:
                            u = t_of[li, it, i]
                            e.wait_ge(q["s_bd"], of_block[w, i] + c)
                            e.activation(aring[:, slot, i - pl.chunks[kc][0], :], psT[u % 2][:], ACT.Copy).then_inc(q["s_tA"], 1)
                    elif it[0] == "L":
                        m = len(it[1])
                        e.wait_ge(q["s_sq"], lb + 1)
                        e.activation(sd[:, 0:m], mv[:, 0:m, 1], ACT.Sqrt, bias=epst[:, 0:1]).then_inc(q["s_sd"], 1)
                        lb += 1

        def x_parts(e, li, it, who):
            b = it[1]
            ks = list(range(4 * b, min(4 * b + 4, NB)))
            if who:
                if li == 0:
                    parts = len(z_parts(ks))
                    before = sum(len(z_parts(list(range(4 * c, min(4 * c + 4, NB))))) for c in range(b % W, b, W))
                    e.wait_ge(q["s_tev"], 4)
                    e.wait_ge(s_xs[b % W], 16 * (before + parts))
                else:
                    e.wait_ge(q["s_st"], NB + (li - 1) * NX + b + 1)
                    e.wait_ge(q["s_dn"], li * W * NCH)
            found = []
            t1 = yst[:, b % 2, :] if li == 0 else left[:, (b % 2) * 4 * P:(b % 2 + 1) * 4 * P]
            for a, c, rr in z_parts(ks):
                if li == 0:
                    s_in = cinv[0:rr, b % W, a * P:c * P]
                else:
                    s_in = psT[t_of[li, it] % 2][0:rr, a * P:c * P]
                found.append((a, c, rr, lambda s, a=a, c=c, rr=rr: xs[0:rr, s, ks[a]:ks[a] + c - a, :].rearrange("p k f -> p (k f)"),
                              s_in, t1[0:rr, a * P:c * P]))
            return found

        def vector_engine(e):
            done = [0]

            def link(ins):
                done[0] += 1
                ins.then_inc(q["s_v2"], 1)
                e.wait_ge(q["s_v2"], done[0])

            def ready():
                e.sem_inc(q["s_v"], 1)

            def cols(c, nth):
                e.wait_ge(q["s_tp"], nth + 1)
                cv = c[:].rearrange("p (t q) -> p q t", q=8)
                for hh in range(2):
                    last = e.tensor_copy(cv[:, 4 * hh:4 * hh + 4, :],
                                         psC[hh][:, 0:4 * NP].rearrange("p (q t) -> p q t", q=4))
                last.then_inc(q["s_tev"], 1)

            taken = [0]

            def small_there():
                taken[0] += 1
                e.wait_ge(q["s_small"], taken[0])

            e.memset(recs[:], -1.0).then_inc(q["s_rf"], 1)
            e.memset(onesf[:], 1.0)
            e.memset(epst[:], EPS)
            e.memset(carry[:], 0.0)
            e.memset(viol[:], 0.0)
            e.memset(mv[:], 1.0)
            e.memset(B[0][:, N:NW], 0.0)
            link(e.memset(B[1][:, N:NW], 0.0))
            e.wait_ge(q["s_e0"], N_E0)
            link(e.scalar_tensor_tensor(a_idx, a_src, float(NR), a_typ, ALU.mult, ALU.add))
            ready()
            cols(idxc, 0)
            e.wait_ge(q["s_tev"], 1)
            link(e.tensor_scalar(blk[:], idxc[:, 0:TH], 9, None, ALU.arith_shift_right))
            onesb = onesf[:, 0:1]

            def rank(i):
                ws = pl.phases[i]
                c0, c1 = 4 * pl.win[ws[0]][0], 4 * pl.win[ws[-1]][1]
                n = c1 - c0
                m = m8[:, 0:NB * n]
                m3 = m.rearrange("p (b t) -> p b t", t=n)
                link(e.memset(sc[:, 0:1], 0.0))
                link(e.tensor_tensor(m3, blk[:, c0:c1].unsqueeze(1).to_broadcast([P, NB, n]),
                                     iota[:, 0:NB].unsqueeze(2).to_broadcast([P, NB, n]), ALU.is_equal))
                link(e.tensor_tensor_scan(sc[:, 1:1 + NB * n], onesb.to_broadcast([P, NB * n]), m, 0.0, ALU.mult, ALU.add))
                before = sc[:, 0:NB * n].rearrange("p (b t) -> p b t", t=n)
                behind = sc[:, 1:1 + NB * n].rearrange("p (b t) -> p b t", t=n)
                for w in ws:
                    a, b = 4 * pl.win[w][0] - c0, 4 * pl.win[w][1] - c0
                    link(e.tensor_tensor(tot[:, w, :], behind[:, :, b - 1], before[:, :, a], ALU.subtract))
                    link(e.tensor_tensor(offs[:, w, :], bucket[:, 0, w * NB:(w + 1) * NB], before[:, :, a], ALU.subtract))
                if i == 0:
                    e.wait_ge(q["s_e1"], N_E1)
                    link(e.tensor_copy(a_dstf, a_dst))
                    ready()
                    dv = a_dst.rearrange("p (h j) -> p h j", h=2)
                    link(e.tensor_copy(chk[:, 5:7], dv[:, :, 0]))
                    for h in range(2):
                        o = 512 * h
                        link(e.scalar_tensor_tensor(a_rel[:, o:o + 512], a_dst[:, o:o + 512], chk[:, 5 + h:6 + h],
                                                    valid[:, o:o + 512], ALU.subtract, ALU.mult))
                    ready()
                    cols(dstc, 1)
                    cols(relc, 2)
                    e.wait_ge(q["s_tev"], 3)
                    ready()
                ready()
                if i == 0:
                    records()
                small_there()
                if i == 0:
                    link(e.tensor_copy(basew[:], psGR[:, 400:400 + W + 1]))
                w0, w1 = ws[0], ws[-1] + 1
                k = (w1 - w0) * NB
                o2 = offs[:, w0:w1, :].rearrange("p w b -> p (w b)")
                t2 = tot[:, w0:w1, :].rearrange("p w b -> p (w b)")
                link(e.tensor_tensor(o2, o2, psGR[:, 0:k], ALU.add))
                e.tensor_tensor(t2, psGR[:, 200:200 + k], bucket[:, 1, w0 * NB:w1 * NB], ALU.subtract).then_inc(q["s_sm"], 1)
                for w in ws:
                    a, b = 4 * pl.win[w][0] - c0, 4 * pl.win[w][1] - c0
                    link(e.tensor_tensor(before[:, :, a:b], before[:, :, a:b],
                                         offs[:, w, :].unsqueeze(2).to_broadcast([P, NB, b - a]), ALU.add))
                link(e.tensor_tensor(before, before, m3, ALU.mult))
                link(e.tensor_reduce(relw[:, c0:c1], sc[:, 0:NB * n].rearrange("p (b t) -> p t b", t=n), AX.X, ALU.add))
                link(e.tensor_copy(posc[:, c0:c1], relw[:, c0:c1]))
                if i == 0:
                    keys()
                e.sem_inc(q["s_pos"], 1)
                if i == 0:
                    link(e.tensor_reduce(viol[:, 1:2], relw[:], AX.X, ALU.max))
                    link(e.tensor_scalar(viol[:, 1:2], viol[:, 1:2], float(P - 1), None, ALU.is_gt))

            def records():
                link(e.tensor_scalar(tmpi[:], idxc[:, 0:TH], 3, None, ALU.bitwise_and))
                link(e.tensor_copy(recv[:, :, 1], tmpi[:]))
                for r in range(NR):
                    link(e.tensor_scalar(tmask[:, :, r], tmpi[:], float(r), None, ALU.is_equal))
                link(e.tensor_scalar(tmpi[:], idxc[:, 0:TH], 2, P - 1, ALU.arith_shift_right, ALU.bitwise_and))
                link(e.tensor_copy(recv[:, :, 0], tmpi[:]))

            def keys():
                link(e.tensor_tensor(delta[:], basew[:, 1:W + 1], basew[:, 0:W], ALU.subtract))
                for w, (a, b, _) in enumerate(pl.win):
                    link(e.tensor_scalar(relw[:, 4 * a:4 * b], dstc[:, 4 * a:4 * b], basew[:, w:w + 1], None, ALU.subtract))
                link(e.scalar_tensor_tensor(recv[:, :, 1], recv[:, :, 1], float(P), relw[:], ALU.mult, ALU.add))

            rank(0)
            for i in range(1, len(pl.phases)):
                rank(i)
            e.wait_ge(q["s_sm"], len(pl.phases))
            link(e.tensor_reduce(viol[:, 2:3], tot[:].rearrange("p w b -> p (w b)"), AX.X, ALU.max))
            link(e.tensor_scalar(viol[:, 2:3], viol[:, 2:3], 0.0, None, ALU.is_gt))
            link(e.tensor_reduce(chk[:, 0:1], a_rel, AX.X, ALU.max))
            link(e.tensor_tensor(fwd, a_prev, a_dst, ALU.subtract))
            link(e.tensor_reduce(chk[:, 1:2], fwd, AX.X, ALU.max))
            link(e.tensor_tensor(need_t[:], need_t[:], chk[:, 5:7], ALU.subtract))
            link(e.tensor_reduce(chk[:, 2:3], need_t[:], AX.X, ALU.max))
            link(e.tensor_tensor(most_t[:], chk[:, 5:7], most_t[:], ALU.subtract))
            link(e.tensor_reduce(chk[:, 3:4], most_t[:], AX.X, ALU.max))
            link(e.tensor_scalar(chk[:, 0:1], chk[:, 0:1], float(P - 1), None, ALU.is_gt))
            link(e.tensor_scalar(chk[:, 1:4], chk[:, 1:4], 0.0, None, ALU.is_gt))
            link(e.tensor_reduce(viol[0:NP, 0:1], chk[:, 0:4], AX.X, ALU.add))
            link(e.tensor_reduce(viol[:, 3:4], viol[:, 0:3], AX.X, ALU.add))
            ready()
            small_there()
            e.tensor_copy(flag_i[:], psGR[0:1, 410:411]).then_inc(q["s_fl"], 1)
            e.tensor_copy(brow[:].rearrange("a h p -> a (h p)"), psGR[0:1, 0:2 * NP]).then_inc(q["s_sm"], 1)

            e.wait_ge(q["s_e2"], N_E2)
            link(e.tensor_tensor(same_p, a_dst, a_prev, ALU.is_equal))
            link(e.tensor_tensor(same_n, a_dst, a_next, ALU.is_equal))
            for r in range(NR):
                if r == 0:
                    link(e.tensor_reduce(ends[:, 0, 0, 0:1], same_p, AX.X, ALU.min))
                    link(e.tensor_reduce(ends[:, 1, 0, 0:1], same_n, AX.X, ALU.min))
                else:
                    link(e.tensor_copy(ends[:, :, 0, r], ends[:, :, 0, 0]))
                link(e.tensor_scalar(mask, a_typ, float(r), None, ALU.is_equal))
                link(e.tensor_tensor_scan(fwd, same_p, mask, 0.0, ALU.mult, ALU.add))
                link(e.tensor_tensor_scan(bwd[:, ::-1], same_n[:, ::-1], mask[:, ::-1], 0.0, ALU.mult, ALU.add))
                link(e.tensor_copy(ends[:, 0, 1, r:r + 1], fwd[:, RW - 1:RW]))
                link(e.tensor_copy(ends[:, 1, 1, r:r + 1], bwd[:, 0:1]))
            ready()
            e.wait_ge(q["s_tp"], 4)
            for d in range(2):
                for w in range(2):
                    link(e.tensor_copy(rowt[:, d, w, 0:NP], psC[d][0:NR, w * NP:(w + 1) * NP]))
            link(e.tensor_tensor_scan(carry[:, 0, 1:NP + 1], rowt[:, 0, 0, 0:NP], rowt[:, 0, 1, 0:NP], 0.0, ALU.mult, ALU.add))
            link(e.tensor_tensor_scan(carry[:, 1, 0:NP][:, ::-1], rowt[:, 1, 0, 0:NP][:, ::-1],
                                      rowt[:, 1, 1, 0:NP][:, ::-1], 0.0, ALU.mult, ALU.add))
            ready()
            e.wait_ge(q["s_tp"], 5)
            for d in range(2):
                link(e.tensor_copy(cin[:, d, :], psC[d][0:NP, 256:256 + NR]))
            link(e.memset(a_w, 1.0))
            for r in range(NR):
                link(e.tensor_scalar(mask, a_typ, float(r), None, ALU.is_equal))
                link(e.tensor_tensor_scan(fwd, same_p, mask, cin[:, 0, r:r + 1], ALU.mult, ALU.add))
                link(e.tensor_tensor_scan(bwd[:, ::-1], same_n[:, ::-1], mask[:, ::-1], cin[:, 1, r:r + 1], ALU.mult, ALU.add))
                link(e.scalar_tensor_tensor(fwd, fwd, -1.0, bwd, ALU.add, ALU.add))
                firsts = [v.rearrange("p (h j) -> p h j", h=2)[:, :, 0] for v in (fwd, mask)]
                e.scalar_tensor_tensor(cfirst[:, :, r], firsts[0], 1.0, firsts[1], ALU.add, ALU.subtract)
                link(e.copy_predicated(a_w, mask.bitcast(I32), fwd))
            link(e.tensor_scalar(a_w, a_w, 1.0, None, ALU.max))
            link(e.reciprocal(a_w, a_w))
            link(e.tensor_tensor(a_w, a_w, valid, ALU.mult))
            ready()
            cols(wc, 5)
            e.wait_ge(q["s_tev"], 4)
            branch(e, "DVE", dve_fast)

        def dve_fast(e):
            done = [0]

            def link(ins):
                done[0] += 1
                ins.then_inc(q["s_v3"], 1)
                e.wait_ge(q["s_v3"], done[0])

            NN = NL * NSG

            def build(n):
                g = sparse[n % NSG]
                if n >= NS:
                    e.wait_ge(q["s_pe"], n - NS + 1)
                for i, t in enumerate(tiles[g]):
                    last = e.tensor_scalar(S[:, n % NS, i, :], iota[:], relc[:, t:t + 1], wc[:, t:t + 1],
                                           ALU.is_equal, ALU.mult)
                last.then_inc(q["s_S"], 1)

            def add(li, it, g, s_part, count):
                _, b = node_src(li)
                v = e.value_load(base_ap[0:1, base_col(g):base_col(g) + 1], min_val=0, max_val=NW - P)
                n = acc_of[li, it]
                e.wait_ge(q["s_rev"], (li + 1) * NB)
                e.wait_ge(q[s_part], count)
                if n > 1:
                    e.wait_ge(q["s_acc"], n - 1)
                w = b[:, bass.ds(v, P)]
                e.tensor_tensor(w, w, part[g_of[li, it] % 2], ALU.add).then_inc(q["s_acc"], 1)

            built = [0]

            def onehots(upto):
                while built[0] < min(upto, len(pairs)):
                    v = built[0]
                    kind, w, i, j = pairs[v]
                    if v == first_of["C", w, 0]:
                        e.wait_ge(q["s_rl"], 16 * (w + 1))
                    if v >= NO:
                        e.wait_ge(q["s_bd"], v - NO + 1)
                    if kind == "A":
                        at = pl.slot0[w] + i * pl.win[w][2] + j
                        e.tensor_scalar(ohs[:, v % NO, :], iota16[:, 0:P], recs[:, at, 0:1], None, ALU.is_equal)
                        last = e.tensor_scalar(ohk[:, v % NO, :], iota16[:], recs[:, at, 1:2], None, ALU.is_equal)
                    else:
                        last = e.tensor_scalar(ohs[:, v % NO, :], iota16[:, 0:P], basew[:, w:w + 1], dstc[:, i:i + 1],
                                               ALU.add, ALU.is_equal)
                    last.then_inc(q["s_oh"], 1)
                    built[0] += 1

            def ahead(pos):
                for it in layers[0][pos:]:
                    if it[0] == "C":
                        onehots(first_of[it] + NO)
                        return
                    if it[0] == "R":
                        return

            def last_stage(b, it):
                ks = it[1]
                z = zx[:, b % NZ]
                u = t_of[NL - 1, it]
                e.wait_ge(q["s_fin"], b + 1)
                e.wait_ge(s_z[b % NZ], z_uses[b][0])
                for a, c, rr in z_parts(ks):
                    last = e.tensor_tensor(z[0:rr, a:c, :], psT[u % 2][0:rr, a * D:c * D].rearrange("p (k f) -> p k f", f=D),
                                           z[0:rr, a:c, :], ALU.add)
                last.then_inc(q["s_tV"], 1)
                e.wait_ge(q["s_tV"], t_uses[u][1])
                if b:
                    e.wait_ge(q["s_sd"], b)
                for j, k in enumerate(ks):
                    last = e.bn_stats(st[0:bw[k], j, :], z[0:bw[k], j, :])
                link(last)
                for j, k in enumerate(ks):
                    last = e.bn_aggr(mv[0:bw[k], j, :], st[0:bw[k], j, :])
                last.then_inc(q["s_sq"], 1)

            def last_stage2(b, it):
                ks = it[1]
                z = zx[:, b % NZ]
                e.wait_ge(q["s_sd"], b + 1)
                link(e.reciprocal(rs[:, 0:len(ks)], sd[:, 0:len(ks)]))
                for j, k in enumerate(ks):
                    rr = bw[k]
                    last = e.tensor_scalar(z[0:rr, j, :], z[0:rr, j, :], mv[0:rr, j, 0:1], rs[0:rr, j:j + 1],
                                           ALU.subtract, ALU.mult)
                last.then_inc(q["s_no"], 1)

            build(0)
            build(1)
            def invert(w):
                link(e.reciprocal(cinv[:, w, :], cinv[:, w, :]))

            lb, pending, uninverted = 0, None, None
            y_stored(e, 0)
            for li, items in enumerate(layers):
                split = set()
                for pos, it in enumerate(items):
                    if pending and it[0] != "C":
                        last_stage2(*pending)
                        pending = None
                    if it[0] == "S":
                        n = li * NSG + it[1]
                        if n + 2 < NN:
                            build(n + 2)
                        if li == 0:
                            ahead(pos)
                        add(li, it, sparse[it[1]], "s_pe", n + 1)
                    elif it[0] == "C" and li == 0:
                        if uninverted is not None:
                            onehots((first_of[it] + first_of[it, "end"]) // 2)
                            invert(uninverted)
                            uninverted = None
                        onehots(first_of[it, "end"])
                    elif it[0] == "N":
                        w = it[1]
                        ahead(pos)
                        e.wait_ge(q["s_bd"], max(v for v, p in enumerate(pairs) if p[0:2] == ("N", w)) + 1)
                        if w:
                            e.wait_ge(q["s_n2"], w)
                        e.tensor_copy(cn[:], psB[0:NR, 0:P]).then_inc(q["s_n1"], 1)
                    elif it[0] == "M":
                        w = it[1]
                        ahead(pos)
                        e.wait_ge(q["s_xw"], NX)
                        e.wait_ge(q["s_cf"], 32)
                        cv = cinv[:, w, :].rearrange("p (r d) -> p r d", r=NR)
                        for r in range(NR):
                            g = starts[w + 1]
                            last = e.tensor_scalar(cv[:, r, :], iota[:], delta[:, w:w + 1],
                                                   cfb[:, g // 2, g % 2, r:r + 1], ALU.is_equal, ALU.mult)
                        link(last)
                        g = starts[w]
                        link(e.tensor_tensor(cv[:, :, 0], cv[:, :, 0], cfb[:, g // 2, g % 2, :], ALU.max))
                        e.wait_ge(q["s_n2"], w + 1)
                        link(e.scalar_tensor_tensor(cinv[:, w, :], psB[:], 1.0, cinv[:, w, :], ALU.max, ALU.max))
                        e.sem_inc(q["s_n3"], 1)
                        uninverted = w
                    elif it[0] == "X":
                        n = x_no[li, it]
                        def first(it):
                            if it not in split:
                                split.add(it)
                                m = x_no[li, it]
                                parts = x_parts(e, li, it, "DVE")
                                e.wait_ge(q["s_xa"], m + 1)
                                if m > 1:
                                    e.wait_ge(q["s_xw"], m - 1)
                                for a, c, rr, o, s_in, t_in in parts:
                                    last = e.tensor_tensor(t_in, s_in, o(0), ALU.subtract)
                                last.then_inc(q["s_xv"], 1)

                        first(it)
                        if items[pos + 1][0] == "X":
                            first(items[pos + 1])
                        e.wait_ge(q["s_xv"], n + 1)
                        e.wait_ge(q["s_xc"], n + 1)
                        for a, c, rr, o, s_in, t_in in x_parts(e, li, it, None):
                            last = e.tensor_tensor(o(2), t_in, o(1), ALU.subtract)
                        last.then_inc(q["s_xw"], 1)
                    elif it[0] == "F":
                        w = it[1]
                        f = f_no[li, it]
                        if li == 0:
                            ahead(pos)
                        if uninverted is not None:
                            invert(uninverted)
                            uninverted = None
                        e.wait_ge(q["s_dn"], chunk_no[li, ("C", w, NCH - 1)] + 1)
                        if f:
                            e.wait_ge(q["s_fp"], f)
                        bank = psD if li == 0 else psC[f % 2]
                        e.tensor_tensor(ms[:], bank[:], cinv[:, w, :], ALU.mult).then_inc(q["s_fd"], 1)
                    elif it[0] == "G":
                        w = it[1]
                        add(li, it, pl.win[w][0], "s_fp", f_no[li, ("F", w)] + 1)
                    elif it[0] == "L":
                        last_stage(lb, it)
                        pending = (lb, it)
                        lb += 1
            if pending:
                last_stage2(*pending)

        steps = []

        def step(who, fn, dma=False):
            steps.append((who, fn, dma))

        def loop(n, body):
            outer = list(steps)
            steps.clear()
            body()
            inner = list(steps)
            steps[:] = outer
            steps.append(("loop", n, inner))
            assert inner[0][0] == "DVE"
            step("DVE", lambda e, i: e.memset(g_junk[:], 0.0))

        g_idx, g_sidx = sb("g_idx", [P, 1], I32), sb("g_sidx", [P, 1], I32)
        g_key, g_pri, g_mul = sb("g_key", [P, 1]), sb("g_pri", [P, 1]), sb("g_mul", [P, 1])
        g_f, g_t, g_w = sb("g_f", [P, 1]), sb("g_t", [P, 1]), sb("g_w", [P, 1])
        g_junk = sb("g_junk", [1, 1])
        g_m, g_ml, g_kb = S[:, 0, 0, :], S[:, 0, 1, :], S[:, 0, 2, :]
        g_x, g_comb = S[:, 1, 0, :], S[:, 1, 1, :]
        keyc = relc

        def dve(fn):
            step("DVE", fn)

        def equal_keys(limit, dump):
            dve(lambda e, i: e.tensor_scalar(g_kb, iota[:], 0.0, g_key[:, 0:1], ALU.mult, ALU.add))
            step("PE", lambda e, i: e.transpose(psT[1][:, 0:P], g_kb, ident[:]))
            dve(lambda e, i: e.tensor_scalar(g_m, psT[1][:, 0:P], g_key[:, 0:1], None, ALU.is_equal))
            dve(lambda e, i: e.tensor_tensor(g_ml, g_m, lower[:], ALU.mult))
            dve(lambda e, i: e.tensor_reduce(g_pri[:], g_ml, AX.X, ALU.add))
            dve(lambda e, i: e.tensor_scalar(g_f[:], g_pri[:], 0.0, None, ALU.is_equal))
            dve(lambda e, i: e.scalar_tensor_tensor(g_f[:], g_key[:], float(limit), g_f[:], ALU.is_lt, ALU.mult))
            dve(lambda e, i: e.scalar_tensor_tensor(g_t[:], g_key[:], dumpc[:, dump:dump + 1], g_f[:], ALU.subtract, ALU.mult))
            dve(lambda e, i: e.tensor_tensor(g_sidx[:], g_t[:], dumpc[:, dump:dump + 1], ALU.add))

        def count_tile():
            dve(lambda e, i: e.tensor_copy(g_key[:], keyc[:, bass.ds(i, 1)]))
            equal_keys(NK, 1)
            dve(lambda e, i: e.tensor_reduce(g_mul[:], g_m, AX.X, ALU.add))
            step("POOL", lambda e, i: e.indirect_dma_start(
                cnt_dram, bass.IndirectOffsetOnAxis(ap=g_sidx[:, 0:1], axis=0), g_mul[:], None,
                compute_op=ALU.add), True)

        def weigh_tile():
            dve(lambda e, i: e.tensor_copy(g_key[:], keyc[:, bass.ds(i, 1)]))
            dve(lambda e, i: e.tensor_scalar(g_idx[:], g_key[:], float(NK - 1), None, ALU.min))
            step("POOL", lambda e, i: e.indirect_dma_start(
                g_mul[:], None, cnt_dram, bass.IndirectOffsetOnAxis(ap=g_idx[:, 0:1], axis=0)), True)
            dve(lambda e, i: e.tensor_scalar(g_mul[:], g_mul[:], 1.0, None, ALU.max))
            dve(lambda e, i: e.reciprocal(g_mul[:], g_mul[:]))
            dve(lambda e, i: e.scalar_tensor_tensor(g_mul[:], g_key[:], float(NK), g_mul[:], ALU.is_lt, ALU.mult))
            dve(lambda e, i: e.tensor_copy(wc[:, bass.ds(i, 1)], g_mul[:]))

        def sum_tile(li):
            dve(lambda e, i: e.tensor_copy(g_idx[:], idxc[:, bass.ds(i, 1)]))
            dve(lambda e, i: e.tensor_copy(g_key[:], dstc[:, bass.ds(i, 1)]))
            dve(lambda e, i: e.tensor_copy(g_w[:], wc[:, bass.ds(i, 1)]))
            step("POOL", lambda e, i: e.indirect_dma_start(
                g_x, None, Y[li % 2], bass.IndirectOffsetOnAxis(ap=g_idx[:, 0:1], axis=0)), True)
            dve(lambda e, i: e.tensor_scalar(g_x, g_x, g_w[:, 0:1], None, ALU.mult))
            equal_keys(N, 0)
            step("PE", lambda e, i: e.matmul(psG, g_m, g_x, start=True, stop=True))
            dve(lambda e, i: e.tensor_copy(g_comb, psG))
            step("POOL", lambda e, i: e.indirect_dma_start(
                acc_dram, bass.IndirectOffsetOnAxis(ap=g_sidx[:, 0:1], axis=0), g_comb, None,
                compute_op=ALU.add), True)

        def general_steps():
            acc3 = acc_dram.rearrange("(k p) f -> p k f", p=P)
            big = ring[:, 0:NB * P].rearrange("p (k f) -> p k f", f=D)
            dve(lambda e, i: e.memset(ring[:], 0.0))
            step("SP", lambda e, i: e.dma_start(cnt_dram.rearrange("(p c) a -> p (c a)", p=P), ring[:, 0:NC]), True)
            dve(lambda e, i: e.tensor_scalar(U[:, 0:NT4].bitcast(I32), idxc[:], NR - 1, None, ALU.bitwise_and))
            dve(lambda e, i: e.scalar_tensor_tensor(keyc[:], dstc[:], float(NR), U[:, 0:NT4].bitcast(I32), ALU.mult, ALU.add))
            loop(NT, count_tile)
            loop(NT, weigh_tile)
            for li in range(NL):
                src_b, acc_b = node_src(li)
                dve(lambda e, i: e.memset(ring[:], 0.0))
                step("SP", lambda e, i: e.dma_start(acc3[:, 0:NB, :], big), True)
                step("SP", lambda e, i: e.dma_start(acc3[:, NB:NB + 1, :], big[:, 0:1, :]), True)
                loop(NT, lambda: sum_tile(li))
                step("SP", lambda e, i: e.dma_start(big, acc3[:, 0:NB, :]), True)
                for k in range(NB):
                    w = bw[k]
                    blk = acc_b[:, P * k:P * k + w]
                    oth = src_b[:, P * k:P * k + w]
                    step("PE", lambda e, i, k=k, w=w: e.transpose(psT[0][:, 0:w], ring[0:w, P * k:P * k + P], ident[0:w, 0:w]))
                    dve(lambda e, i, blk=blk, w=w: e.tensor_tensor(blk, blk, psT[0][:, 0:w], ALU.add))
                    if li < 2:
                        ln = li + 1
                        dve(lambda e, i, blk=blk: e.tensor_scalar(blk, blk, 0.0, None, ALU.max))
                        step("PE", lambda e, i, blk=blk, w=w, ln=ln: e.matmul(
                            psY[0][0:w, :], blk, wt[:, ln].rearrange("i r o -> i (r o)"), start=True, stop=True))
                        dve(lambda e, i, w=w: e.tensor_copy(yst[0:w, 0, :], psY[0][0:w, :]))
                        step("SP", lambda e, i, k=k, w=w, ln=ln: e.dma_start(
                            Y[ln % 2][NR * P * k:NR * (P * k + w), :].rearrange("(n r) f -> n (r f)", r=NR),
                            yst[0:w, 0, :]), True)
                        step("PE", lambda e, i, blk=blk, w=w, ln=ln: e.matmul(
                            psR[:, 0:w], rt[:, ln, :], blk, start=True, stop=True))
                        dve(lambda e, i, oth=oth, w=w, ln=ln: e.tensor_scalar(
                            oth, psR[:, 0:w], bt[:, ln:ln + 1], None, ALU.add))
                    else:
                        z = zx[0:w, 0, 0, :]
                        step("SP", lambda e, i, z=z, k=k, w=w: e.dma_start(z, x[P * k:P * k + w, :]), True)
                        step("PE", lambda e, i, blk=blk, w=w: e.transpose(psT[0][0:w, 0:D], blk, ident[:]))
                        dve(lambda e, i, z=z, k=k, w=w: e.tensor_tensor(z, psT[0][0:w, 0:D], z, ALU.add))
                        dve(lambda e, i, z=z, w=w: e.bn_stats(st[0:w, 0, :], z))
                        dve(lambda e, i, w=w: e.bn_aggr(mv[0:w, 0, :], st[0:w, 0, :]))
                        step("ACT", lambda e, i, w=w: e.activation(sd[0:w, 0:1], mv[0:w, 0, 1:2], ACT.Sqrt, bias=epst[0:w, 0:1]))
                        dve(lambda e, i, w=w: e.reciprocal(rs[0:w, 0:1], sd[0:w, 0:1]))
                        dve(lambda e, i, z=z, w=w: e.tensor_scalar(z, z, mv[0:w, 0, 0:1], rs[0:w, 0:1], ALU.subtract, ALU.mult))
                        step("SP", lambda e, i, z=z, k=k, w=w: e.dma_start(out[P * k:P * k + w, :], z), True)

        general_steps()

        def general(e, name):
            token = {n: q["t" + n] for n in ("SP", "PE", "ACT", "DVE", "POOL")}

            def emit(items, i, follows):
                for n, item in enumerate(items):
                    after_this = items[n + 1] if n + 1 < len(items) else follows
                    if item[0] == "loop":
                        first = item[2][0]
                        if any(s[0] == name for s in item[2]):
                            with e.Fori(0, item[1]) as j:
                                emit(item[2], j, first)
                        continue
                    who, fn, dma = item
                    if who != name:
                        continue
                    e.wait_ge(token[who], 1)
                    e.sem_clear(token[who])
                    to = after_this
                    while to is not None and to[0] == "loop":
                        to = to[2][0]
                    ins = fn(e, i)
                    if dma:
                        landed = q["gd" if name == "SP" else "gp"]
                        ins.then_inc(landed, 16)
                        e.wait_ge(landed, 16)
                        if name == "POOL":
                            e.dma_reset(range(landed.num, landed.num + 1))
                        e.sem_clear(landed)
                        if to is not None:
                            e.sem_inc(token[to[0]], 1)
                    elif to is not None:
                        ins.then_inc(token[to[0]], 1)

            if name == "DVE":
                e.wait_ge(q["s_tev"], 4)
                e.wait_ge(q["s_pf"], 16)
                e.wait_ge(q["s_w1"], 32)
                for n in range(AHEAD):
                    e.wait_ge(s_ring[n], ring_need[n])
                e.wait_ge(s_sc[0], 16 * 4 * (pl.win[0][1] - pl.win[0][0]))
                e.wait_ge(q["s_yev"], NB)
                e.wait_ge(q["s_rev"], NB)
                y_stored(e, 0)
                e.sem_inc(token["DVE"], 1)
            emit(steps, None, None)

        block.sync(sync_engine)
        block.gpsimd(gpsimd_engine)
        block.tensor(tensor_engine)
        block.scalar(scalar_engine)
        block.vector(vector_engine)
    return nc


_INS = ["x", "src", "dst", "edge_type_4", "L0_gnn_weights", "L0_gnn_roots", "L0_gnn_biases"]


def kernel(**inputs):
    import concourse.bacc as _bacc
    from concourse.bass_utils import run_bass_kernel_spmd as _run

    nc = _bacc.Bacc("TRN2", target_bir_lowering=False, num_devices=1)
    arrays, args = {}, []
    given = {n: np.ascontiguousarray(inputs[n]) for n in _INS}
    given.update(constants(given["x"].shape[0], given["src"].shape[0]))
    for name, a in given.items():
        arrays[f"in_{name}"] = a
        args.append(nc.dram_tensor(f"in_{name}", a.shape, mybir.dt.from_np(a.dtype), kind="ExternalInput").ap())
    o = nc.dram_tensor("out_0", given["x"].shape, F32, kind="ExternalOutput").ap()
    rgcn_kernel(nc, *args, o)
    r = _run(nc, [arrays], core_ids=[0])
    return r.results[0]["out_0"]
```
